# Optimizing a Trainium2 kernel written in Bass

```python
import numpy as np
import jax
import jax.numpy as jnp

def _softmax(x, axis=-1):
    return jax.nn.softmax(x, axis=axis)

def _gelu(x):
    return jax.nn.gelu(x, approximate=True)

def _silu(x):
    return jax.nn.silu(x)

def _sigmoid(x):
    return jax.nn.sigmoid(x)

def _layernorm(x, axis=-1, eps=1e-05):
    m = jnp.mean(x, axis=axis, keepdims=True)
    v = jnp.var(x, axis=axis, keepdims=True)
    return (x - m) / jnp.sqrt(v + eps)

def _scatter_add(tgt, idx, src, axis=0):
    return tgt.at[idx].add(src)

def _segment_sum(src, seg, n):
    return jax.ops.segment_sum(src, seg, n)
kernel_name = 'mk_decoder_preln_d1_seqx_r8_f648f7'

def setup_inputs(seed: int=0):
    np.random.seed(seed)
    _w = jnp.asarray

    def _rec_inputs():
        import jax
        import jax.numpy as jnp
        _rk = jax.random.key(seed)
        x = -0.0005857 + 0.9999 * jax.random.normal(jax.random.fold_in(_rk, 1), (16, 56, 128), jnp.float32)
        _lenS = 56 - jax.random.randint(jax.random.fold_in(_rk, 7), (16,), 0, max(1, 56 // 4) + 1, jnp.int32)
        _lenS2 = 1500 - jax.random.randint(jax.random.fold_in(_rk, 8), (16,), 0, max(1, 1500 // 4) + 1, jnp.int32)
        _ctx_1024P = jax.random.normal(jax.random.fold_in(_rk, 11), (16, 16, 128), jnp.float32)
        _ctx_1024c = jax.random.dirichlet(jax.random.fold_in(_rk, 511), 0.3 * jnp.ones((16,), jnp.float32), (16, 1500))
        _ctx_1024t = jnp.einsum('bsk,bkd->bsd', _ctx_1024c, _ctx_1024P)
        _ctx_1024t = _ctx_1024t * jax.lax.rsqrt(jnp.mean(jnp.square(_ctx_1024t)) + 1e-12) * 0.953939
        ctx_1024 = -0.000264403 + 1.00002 * (_ctx_1024t + 0.3 * jax.random.normal(jax.random.fold_in(_rk, 611), (16, 1500, 128), jnp.float32))
        _validS = jnp.arange(56)[None, :] < _lenS[:, None]
        _validS2 = jnp.arange(1500)[None, :] < _lenS2[:, None]
        _causal = jnp.tril(jnp.ones((56, 56), dtype=bool))
        mask_1x1xSxS2_if1 = jnp.where(jnp.ones((1, 1, 56, 1500), dtype=bool), 1, 0).astype(jnp.int32)
        return (x, ctx_1024, mask_1x1xSxS2_if1)
    x, ctx_1024, mask_1x1xSxS2_if1 = _rec_inputs()

    def _L0_attn_setup():
        import jax, jax.numpy as jnp
        import numpy as np
        D_MODEL = 128
        D_STATE = 64
        D_CONV = 4
        EXPAND = 2
        HEADDIM = 128
        NGROUPS = 1
        D_INNER = EXPAND * D_MODEL
        NHEADS = D_INNER // HEADDIM
        CONV_DIM = D_INNER + 2 * NGROUPS * D_STATE
        D_IN_PROJ = 2 * D_INNER + 2 * NGROUPS * D_STATE + NHEADS
        BATCH, SEQLEN = (2, 256)
        DT_MIN, DT_MAX, DT_FLOOR = (0.001, 0.1, 0.0001)
        RMS_EPS = 1e-05

        def _mamba2_forward(u, in_proj_w, conv_w, conv_b, dt_bias, A_log, D_param, norm_w, out_proj_w):
            B, L, _ = u.shape
            zxbcdt = jnp.einsum('bld,ed->ble', u, in_proj_w)
            z = zxbcdt[..., :D_INNER]
            xBC = zxbcdt[..., D_INNER:D_INNER + CONV_DIM]
            dt = jax.nn.softplus(zxbcdt[..., D_INNER + CONV_DIM:] + dt_bias)
            xc = jnp.swapaxes(xBC, 1, 2)
            xc = jax.lax.conv_general_dilated(xc, conv_w, window_strides=(1,), padding=[(D_CONV - 1, 0)], feature_group_count=CONV_DIM)
            xc = jax.nn.silu(xc + conv_b[None, :, None])
            xBC = jnp.swapaxes(xc, 1, 2)
            x = xBC[..., :D_INNER].reshape(B, L, NHEADS, HEADDIM)
            Bmat = xBC[..., D_INNER:D_INNER + D_STATE]
            Cmat = xBC[..., D_INNER + D_STATE:]
            A = -jnp.exp(A_log)

            def step(state, inp):
                dt_t, x_t, B_t, C_t = inp
                dA = jnp.exp(dt_t * A)[:, :, None, None]
                state = state * dA + dt_t[:, :, None, None] * x_t[:, :, :, None] * B_t[:, None, None, :]
                y_t = jnp.einsum('bhpn,bn->bhp', state, C_t) + D_param[None, :, None] * x_t
                return (state, y_t)
            state0 = jnp.zeros((B, NHEADS, HEADDIM, D_STATE), u.dtype)
            inputs = (jnp.moveaxis(dt, 1, 0), jnp.moveaxis(x, 1, 0), jnp.moveaxis(Bmat, 1, 0), jnp.moveaxis(Cmat, 1, 0))
            _, ys = jax.lax.scan(step, state0, inputs)
            y = jnp.moveaxis(ys, 0, 1).reshape(B, L, D_INNER)
            yg = y * jax.nn.silu(z)
            rms = jax.lax.rsqrt(jnp.mean(yg * yg, axis=-1, keepdims=True) + RMS_EPS)
            yn = yg * rms * norm_w
            return jnp.einsum('ble,de->bld', yn, out_proj_w)
        key = jax.random.key(seed)
        ks = jax.random.split(key, 8)
        u = jax.random.normal(ks[0], (BATCH, SEQLEN, D_MODEL), jnp.float32)
        in_proj_w = jax.random.normal(ks[1], (D_IN_PROJ, D_MODEL), jnp.float32) * 0.02
        conv_w = jax.random.normal(ks[2], (CONV_DIM, 1, D_CONV), jnp.float32) * 0.2
        conv_b = jax.random.normal(ks[3], (CONV_DIM,), jnp.float32) * 0.02
        dt = jnp.exp(jax.random.uniform(ks[4], (NHEADS,)) * (jnp.log(DT_MAX) - jnp.log(DT_MIN)) + jnp.log(DT_MIN))
        dt = jnp.maximum(dt, DT_FLOOR)
        dt_bias = dt + jnp.log(-jnp.expm1(-dt))
        A_log = jnp.log(jax.random.uniform(ks[5], (NHEADS,), minval=1.0, maxval=16.0))
        D_param = jnp.ones((NHEADS,), jnp.float32)
        norm_w = jnp.ones((D_INNER,), jnp.float32)
        out_proj_w = jax.random.normal(ks[6], (D_MODEL, D_INNER), jnp.float32) * 0.02
        return {'u': u, 'in_proj_w': in_proj_w, 'conv_w': conv_w, 'conv_b': conv_b, 'dt_bias': dt_bias, 'A_log': A_log, 'D_param': D_param, 'norm_w': norm_w, 'out_proj_w': out_proj_w}
    _L0_attn_all = _L0_attn_setup()
    _L0_attn_in = {k: v for k, v in _L0_attn_all.items() if k in ('in_proj_w', 'conv_w', 'conv_b', 'dt_bias', 'A_log', 'D_param', 'norm_w', 'out_proj_w')}
    del _L0_attn_all

    def _L0_xattn_setup():
        import jax, jax.numpy as jnp
        import numpy as np
        B, S, D, H = (2, 256, 128, 16)
        DK = D // H
        key = jax.random.key(seed)
        ks = jax.random.split(key, 8)

        def lin(k):
            kw, kb = jax.random.split(k)
            w = jax.random.normal(kw, (D, D), dtype=jnp.float32) / np.sqrt(D)
            b = jax.random.normal(kb, (D,), dtype=jnp.float32) * 0.01
            return (w, b)
        wq, bq = lin(ks[0])
        wk, bk = lin(ks[1])
        wv, bv = lin(ks[2])
        wo, bo = lin(ks[3])
        return {'q': jax.random.normal(ks[4], (B, S, D), dtype=jnp.float32), 'k': jax.random.normal(ks[5], (B, S, D), dtype=jnp.float32), 'v': jax.random.normal(ks[6], (B, S, D), dtype=jnp.float32), 'mask': jnp.ones((1, 1, S, S), dtype=jnp.int32), 'wq': wq, 'bq': bq, 'wk': wk, 'bk': bk, 'wv': wv, 'bv': bv, 'wo': wo, 'bo': bo}
    _L0_xattn_all = _L0_xattn_setup()
    _L0_xattn_in = {k: v for k, v in _L0_xattn_all.items() if k in ('wq', 'bq', 'wk', 'bk', 'wv', 'bv', 'wo', 'bo')}
    del _L0_xattn_all

    def _L0_ffn_setup():
        import jax, jax.numpy as jnp
        import numpy as np
        EPS = 1e-05
        TOP_K = 2

        def _rmsnorm(x, w):
            xf = x.astype(jnp.float32)
            rms = jax.lax.rsqrt(jnp.mean(xf * xf, axis=-1, keepdims=True) + EPS)
            return (xf * rms).astype(x.dtype) * w

        def _attention(x, wq, wk, wv, wo, num_heads=16):
            B, S, H = x.shape
            D = H // num_heads
            q = (x @ wq.T).reshape(B, S, num_heads, D)
            k = (x @ wk.T).reshape(B, S, num_heads, D)
            v = (x @ wv.T).reshape(B, S, num_heads, D)
            scale = 1.0 / jnp.sqrt(jnp.float32(D)).astype(x.dtype)
            scores = jnp.einsum('bqhd,bkhd->bhqk', q, k) * scale
            probs = jax.nn.softmax(scores, axis=-1)
            out = jnp.einsum('bhqk,bkhd->bqhd', probs, v).reshape(B, S, H)
            return out @ wo.T

        def _moe(x, gate_w, w1, w2, w3):
            B, S, H = x.shape
            xf = x.reshape(-1, H)
            logits = xf @ gate_w.T
            rw, sel = jax.lax.top_k(logits, TOP_K)
            rw = jax.nn.softmax(rw.astype(jnp.float32), axis=-1).astype(x.dtype)
            E = gate_w.shape[0]
            out = jnp.zeros_like(xf)
            for e in range(E):
                we = jnp.sum(jnp.where(sel == e, rw, 0.0), axis=-1)
                h = jax.nn.silu(xf @ w1[e].T) * (xf @ w3[e].T)
                out = out + h @ w2[e].T * we[:, None]
            return out.reshape(B, S, H)
        key = jax.random.key(seed)
        ks = jax.random.split(key, 10)
        H, I, E, NH = (128, 256, 8, 16)
        B, S = (2, 256)
        s = 0.02
        return {'x': jax.random.normal(ks[0], (B, S, H), jnp.float32), 'ln1_w': jnp.ones((H,), jnp.float32), 'ln2_w': jnp.ones((H,), jnp.float32), 'wq': jax.random.normal(ks[1], (H, H), jnp.float32) * s, 'wk': jax.random.normal(ks[2], (H, H), jnp.float32) * s, 'wv': jax.random.normal(ks[3], (H, H), jnp.float32) * s, 'wo': jax.random.normal(ks[4], (H, H), jnp.float32) * s, 'gate_w': jax.random.normal(ks[5], (E, H), jnp.float32) * s, 'w1': jax.random.normal(ks[6], (E, I, H), jnp.float32) * s, 'w2': jax.random.normal(ks[7], (E, H, I), jnp.float32) * s, 'w3': jax.random.normal(ks[8], (E, I, H), jnp.float32) * s}
    _L0_ffn_all = _L0_ffn_setup()
    _L0_ffn_in = {k: v for k, v in _L0_ffn_all.items() if k in ('ln1_w', 'ln2_w', 'wq', 'wk', 'wv', 'wo', 'gate_w', 'w1', 'w2', 'w3')}
    del _L0_ffn_all
    return {'x': x, 'ctx_1024': ctx_1024, 'mask_1x1xSxS2_if1': mask_1x1xSxS2_if1, 'L0_attn_in_proj_w': _L0_attn_in['in_proj_w'], 'L0_attn_conv_w': _L0_attn_in['conv_w'], 'L0_attn_conv_b': _L0_attn_in['conv_b'], 'L0_attn_dt_bias': _L0_attn_in['dt_bias'], 'L0_attn_A_log': _L0_attn_in['A_log'], 'L0_attn_D_param': _L0_attn_in['D_param'], 'L0_attn_norm_w': _L0_attn_in['norm_w'], 'L0_attn_out_proj_w': _L0_attn_in['out_proj_w'], 'L0_xattn_wq': _L0_xattn_in['wq'], 'L0_xattn_bq': _L0_xattn_in['bq'], 'L0_xattn_wk': _L0_xattn_in['wk'], 'L0_xattn_bk': _L0_xattn_in['bk'], 'L0_xattn_wv': _L0_xattn_in['wv'], 'L0_xattn_bv': _L0_xattn_in['bv'], 'L0_xattn_wo': _L0_xattn_in['wo'], 'L0_xattn_bo': _L0_xattn_in['bo'], 'L0_ffn_ln1_w': _L0_ffn_in['ln1_w'], 'L0_ffn_ln2_w': _L0_ffn_in['ln2_w'], 'L0_ffn_wq': _L0_ffn_in['wq'], 'L0_ffn_wk': _L0_ffn_in['wk'], 'L0_ffn_wv': _L0_ffn_in['wv'], 'L0_ffn_wo': _L0_ffn_in['wo'], 'L0_ffn_gate_w': _L0_ffn_in['gate_w'], 'L0_ffn_w1': _L0_ffn_in['w1'], 'L0_ffn_w2': _L0_ffn_in['w2'], 'L0_ffn_w3': _L0_ffn_in['w3']}

def reference(x, ctx_1024, mask_1x1xSxS2_if1, L0_attn_in_proj_w, L0_attn_conv_w, L0_attn_conv_b, L0_attn_dt_bias, L0_attn_A_log, L0_attn_D_param, L0_attn_norm_w, L0_attn_out_proj_w, L0_xattn_wq, L0_xattn_bq, L0_xattn_wk, L0_xattn_bk, L0_xattn_wv, L0_xattn_bv, L0_xattn_wo, L0_xattn_bo, L0_ffn_ln1_w, L0_ffn_ln2_w, L0_ffn_wq, L0_ffn_wk, L0_ffn_wv, L0_ffn_wo, L0_ffn_gate_w, L0_ffn_w1, L0_ffn_w2, L0_ffn_w3):
    import jax
    import jax.numpy as jnp

    def _L0_attn_ref(u, in_proj_w, conv_w, conv_b, dt_bias, A_log, D_param, norm_w, out_proj_w):
        import jax, jax.numpy as jnp
        import numpy as np
        D_MODEL = 128
        D_STATE = 64
        D_CONV = 4
        EXPAND = 2
        HEADDIM = 128
        NGROUPS = 1
        D_INNER = EXPAND * D_MODEL
        NHEADS = D_INNER // HEADDIM
        CONV_DIM = D_INNER + 2 * NGROUPS * D_STATE
        D_IN_PROJ = 2 * D_INNER + 2 * NGROUPS * D_STATE + NHEADS
        BATCH, SEQLEN = (2, 256)
        DT_MIN, DT_MAX, DT_FLOOR = (0.001, 0.1, 0.0001)
        RMS_EPS = 1e-05

        def _mamba2_forward(u, in_proj_w, conv_w, conv_b, dt_bias, A_log, D_param, norm_w, out_proj_w):
            B, L, _ = u.shape
            zxbcdt = jnp.einsum('bld,ed->ble', u, in_proj_w)
            z = zxbcdt[..., :D_INNER]
            xBC = zxbcdt[..., D_INNER:D_INNER + CONV_DIM]
            dt = jax.nn.softplus(zxbcdt[..., D_INNER + CONV_DIM:] + dt_bias)
            xc = jnp.swapaxes(xBC, 1, 2)
            xc = jax.lax.conv_general_dilated(xc, conv_w, window_strides=(1,), padding=[(D_CONV - 1, 0)], feature_group_count=CONV_DIM)
            xc = jax.nn.silu(xc + conv_b[None, :, None])
            xBC = jnp.swapaxes(xc, 1, 2)
            x = xBC[..., :D_INNER].reshape(B, L, NHEADS, HEADDIM)
            Bmat = xBC[..., D_INNER:D_INNER + D_STATE]
            Cmat = xBC[..., D_INNER + D_STATE:]
            A = -jnp.exp(A_log)

            def step(state, inp):
                dt_t, x_t, B_t, C_t = inp
                dA = jnp.exp(dt_t * A)[:, :, None, None]
                state = state * dA + dt_t[:, :, None, None] * x_t[:, :, :, None] * B_t[:, None, None, :]
                y_t = jnp.einsum('bhpn,bn->bhp', state, C_t) + D_param[None, :, None] * x_t
                return (state, y_t)
            state0 = jnp.zeros((B, NHEADS, HEADDIM, D_STATE), u.dtype)
            inputs = (jnp.moveaxis(dt, 1, 0), jnp.moveaxis(x, 1, 0), jnp.moveaxis(Bmat, 1, 0), jnp.moveaxis(Cmat, 1, 0))
            _, ys = jax.lax.scan(step, state0, inputs)
            y = jnp.moveaxis(ys, 0, 1).reshape(B, L, D_INNER)
            yg = y * jax.nn.silu(z)
            rms = jax.lax.rsqrt(jnp.mean(yg * yg, axis=-1, keepdims=True) + RMS_EPS)
            yn = yg * rms * norm_w
            return jnp.einsum('ble,de->bld', yn, out_proj_w)
        return _mamba2_forward(u, in_proj_w, conv_w, conv_b, dt_bias, A_log, D_param, norm_w, out_proj_w)

    def _L0_xattn_ref(q, k, v, mask, wq, bq, wk, bk, wv, bv, wo, bo):
        import jax, jax.numpy as jnp
        import numpy as np
        B, S, D, H = (2, 256, 128, 16)
        DK = D // H
        b, s, _ = q.shape
        Q = (q @ wq.T + bq).reshape(b, s, H, DK).transpose(0, 2, 1, 3)
        K = (k @ wk.T + bk).reshape(b, -1, H, DK).transpose(0, 2, 1, 3)
        V = (v @ wv.T + bv).reshape(b, -1, H, DK).transpose(0, 2, 1, 3)
        scores = jnp.einsum('bhqd,bhkd->bhqk', Q, K) / np.sqrt(DK)
        scores = jnp.where(mask == 0, jnp.float32(-1e-09), scores)
        att = jax.nn.softmax(scores, axis=-1)
        x = jnp.einsum('bhqk,bhkd->bhqd', att, V)
        x = x.transpose(0, 2, 1, 3).reshape(b, s, H * DK)
        return x @ wo.T + bo

    def _L0_ffn_ref(x, ln1_w, ln2_w, wq, wk, wv, wo, gate_w, w1, w2, w3):
        import jax, jax.numpy as jnp
        import numpy as np
        EPS = 1e-05
        TOP_K = 2

        def _rmsnorm(x, w):
            xf = x.astype(jnp.float32)
            rms = jax.lax.rsqrt(jnp.mean(xf * xf, axis=-1, keepdims=True) + EPS)
            return (xf * rms).astype(x.dtype) * w

        def _attention(x, wq, wk, wv, wo, num_heads=16):
            B, S, H = x.shape
            D = H // num_heads
            q = (x @ wq.T).reshape(B, S, num_heads, D)
            k = (x @ wk.T).reshape(B, S, num_heads, D)
            v = (x @ wv.T).reshape(B, S, num_heads, D)
            scale = 1.0 / jnp.sqrt(jnp.float32(D)).astype(x.dtype)
            scores = jnp.einsum('bqhd,bkhd->bhqk', q, k) * scale
            probs = jax.nn.softmax(scores, axis=-1)
            out = jnp.einsum('bhqk,bkhd->bqhd', probs, v).reshape(B, S, H)
            return out @ wo.T

        def _moe(x, gate_w, w1, w2, w3):
            B, S, H = x.shape
            xf = x.reshape(-1, H)
            logits = xf @ gate_w.T
            rw, sel = jax.lax.top_k(logits, TOP_K)
            rw = jax.nn.softmax(rw.astype(jnp.float32), axis=-1).astype(x.dtype)
            E = gate_w.shape[0]
            out = jnp.zeros_like(xf)
            for e in range(E):
                we = jnp.sum(jnp.where(sel == e, rw, 0.0), axis=-1)
                h = jax.nn.silu(xf @ w1[e].T) * (xf @ w3[e].T)
                out = out + h @ w2[e].T * we[:, None]
            return out.reshape(B, S, H)
        h = x + _attention(_rmsnorm(x, ln1_w), wq, wk, wv, wo)
        h = h + _moe(_rmsnorm(h, ln2_w), gate_w, w1, w2, w3)
        return h
    x = x + _L0_attn_ref(_layernorm(x, axis=-1), L0_attn_in_proj_w, L0_attn_conv_w, L0_attn_conv_b, L0_attn_dt_bias, L0_attn_A_log, L0_attn_D_param, L0_attn_norm_w, L0_attn_out_proj_w)
    x = x + _L0_xattn_ref(_layernorm(x, axis=-1), ctx_1024, ctx_1024, mask_1x1xSxS2_if1, L0_xattn_wq, L0_xattn_bq, L0_xattn_wk, L0_xattn_bk, L0_xattn_wv, L0_xattn_bv, L0_xattn_wo, L0_xattn_bo)
    x = x + _L0_ffn_ref(_layernorm(x, axis=-1), L0_ffn_ln1_w, L0_ffn_ln2_w, L0_ffn_wq, L0_ffn_wk, L0_ffn_wv, L0_ffn_wo, L0_ffn_gate_w, L0_ffn_w1, L0_ffn_w2, L0_ffn_w3)
    return x

_drawn_inputs = setup_inputs


def setup_inputs(seed=0):
    import zlib

    import numpy as np

    out = dict(_drawn_inputs(seed))
    spreads = {'L0_attn_D_param': (1.0, 0.6),
     'L0_attn_norm_w': (1.0, 0.2),
     'L0_ffn_ln1_w': (1.0, 0.6),
     'L0_ffn_ln2_w': (1.0, 0.6)}
    factors = {'L0_attn_dt_bias': 8.0,
     'L0_attn_A_log': 8.0,
     'L0_xattn_bq': 8.0,
     'L0_xattn_bk': 8.0,
     'L0_xattn_bv': 7.034,
     'L0_xattn_bo': 6.283,
     'L0_ffn_wq': 8.0,
     'L0_ffn_wk': 8.0,
     'L0_ffn_wv': 5.096,
     'L0_ffn_wo': 4.977,
     'L0_ffn_gate_w': 8.0,
     'L0_ffn_w1': 8.0,
     'L0_ffn_w2': 8.0,
     'L0_ffn_w3': 8.0}
    for name, (base, spread) in spreads.items():
        noise = np.random.default_rng([zlib.crc32(name.encode()), seed]).standard_normal(out[name].shape)
        drawn = base * np.exp(spread * noise) if base else spread * noise
        out[name] = jnp.asarray(drawn.astype(out[name].dtype))
    for name, factor in factors.items():
        out[name] = (out[name] * factor).astype(out[name].dtype)
    return out
```

```python
from contextlib import ExitStack

import concourse.bass as bass
from concourse import mybir

ALU = mybir.AluOpType
ACT = mybir.ActivationFunctionType
AX = mybir.AxisListType.X
F32 = mybir.dt.float32
F32R = mybir.dt.float32r
I32 = mybir.dt.int32
U32 = mybir.dt.uint32
U8 = mybir.dt.uint8

D = 128
B, S = 16, 56
TOK = B * S
PT = 2 * S
NP = B // 2
HALF = TOK // 2
CTX = 1500
CK = 125
NC = CTX // CK
KB = 500
NKB = CTX // KB
H, DK = 16, 8
GH = 4
NG = H // GH
GR = GH * DK
GQ = GH * S
STK = 3 * GR + 1
HQ = H * S
NT = HQ // 128
NU = NT * NKB
VH = DK + 1
VC = VH * (H + 2)
PVC = 5 * S
EPS = 1e-5
MASKED = -1e-9
DI, DS, HD = 256, 64, 128
MH = DI // HD
CONV = DI + 2 * DS
TAPS = 4
NE, FI = 8, 256
NF = FI // 128
SCALE = float(DK) ** -0.5
VGROUPS = [(t, VH * 3 * t, 3 * S * t, 3, 0) for t in range(4)] + \
          [(t, VH * (12 + 2 * t), S * (12 + 2 * t), 2, 3 * S) for t in range(2)]
ROW_STEPS = (9, 11)
VALUE_PARTS = [(slice(0, 128), slice(0, 3 * S)), (slice(0, 64), slice(3 * S, PVC))]


def widths(**kw):
    at, n = {}, 0
    for name, k in kw.items():
        at[name] = (n, k)
        n += k
    return at, n


CST, CST_N = widths(ident=128, spread=128, block=PVC, heads=H, groups=GH, start=PT, half=128, expert=NE)
MW, MW_N = widths(w_in=2 * DI + 2 * DS + MH, w_out=2 * D, norm=2, conv_b=1)
XW, XW_N = widths(wk=D, wv=D, bk=1, wo=2 * D, bv=2, wq3=NG * 3 * GR, wq=D, bq3=NG, bq=1)
FW, FW_N = widths(wq=D, wk=D, wv=D, wo=2 * D, gate=NE, ln1=1, ln2=1, w1=NE * FI, w3=NE * FI, w2=NE * NF * D)


class Batch:

    def __init__(self, reg, k):
        self.reg, self.k, self.parity = reg, k, k % 2

    def plus(self, n):
        return Batch(self.reg, self.k + n)

    def count(self, per, more=0):
        c = self.k * per + more
        return c if self.reg is None else self.reg * (2 * per) + c

    def buffer_count(self, per):
        c = (self.k // 2 + 1) * per
        return c if self.reg is None else self.reg * per + c

    def within(self, last):
        return self.reg is not None or 0 <= self.k < last


def wait(eng, sem, value):
    if not isinstance(value, int) or value > 0:
        eng.wait_ge(sem, value)


def in_register(eng, value):
    return value if isinstance(value, int) else eng.to_reg(value)


def build(nc, x, ctx_t, mask_t, mask_rows, cst_d, mw_d, xw_d, fw_d, conv_w, small, rows, out):
    es, context, early, query, cross, late = (ExitStack() for _ in range(6))
    with es:
        def sb(name, shape, dt=F32, where=es):
            return where.enter_context(nc.sbuf_tensor(name, shape, dt))

        def pb(name, shape):
            return es.enter_context(nc.psum_tensor(name, shape, F32))

        def sem(name):
            return es.enter_context(nc.semaphore(name))

        st = [pb(f"st{i}", [128, 2, 512]) for i in range(2)]
        mx = [pb(f"mx{i}", [128, 512]) for i in range(2)]
        pv = pb("pv", [128, 512])
        ms = pb("ms", [128, 512])

        cst = sb("cst", [128, CST_N])
        ident, spread, block_mask, head_mask, group_mask, start_ident, half_rows, expert_id = (
            cst[:, a:a + n] for a, n in CST.values())
        ident_r = sb("ident_r", [128, 128], F32R)
        half_r = sb("half_r", [2, 128], F32R)
        ones = sb("ones", [128, 128])
        eps_col = sb("eps_col", [128, 1])
        xw = sb("xw", [128, XW_N])
        wk_t, wv_t, bk_col, wo_rows, bv_rows, wq3, wq_t, bq3, bq_col = (xw[:, a:a + n] for a, n in XW.values())
        bq_s = sb("bq_s", [128, NG + 1])
        masked_col = sb("masked_col", [128, 1])
        key_masked = sb("key_masked", [CK, NC, S], U8)
        any_masked, flag = sb("any_masked", [CK, 1]), sb("flag", [1, 1], I32)
        row_sb = sb("row_sb", [1, DI + D])
        fw = sb("fw", [128, FW_N])
        fwq, fwk, fwv, fwo, gate_t, ln1, ln2, w1_t, w3_t, w2_t = (fw[:, a:a + n] for a, n in FW.values())
        x_sb = sb("x_sb", [PT, NP, D])
        stats, mv = sb("stats", [PT, NP, 6]), sb("mv", [PT, NP, 2])
        lnv, rstd, ssum = sb("lnv", [PT, NP]), sb("rstd", [PT, NP]), sb("ssum", [PT, NP])
        o_all = sb("o_all", [128, 2, TOK])

        ctx_sb = [sb(f"ctx{i}", [D, CTX], where=context) for i in range(2)]
        k_hi = [sb(f"k_hi{i}", [D, CTX], F32R, context) for i in range(2)]
        k_lo = [sb(f"k_lo{i}", [D, CTX], F32R, context) for i in range(2)]
        k_stack = [sb("k_stack0", [STK, NG, CTX], F32R, context), None]
        v_sb = [sb("v0", [CK, NC, VC], where=context), None]

        key_mask = sb("key_mask", [CK, NC, S], I32, early)
        mw = sb("mw", [128, MW_N], where=early)
        w_in, w_out, norm_w, conv_b = (mw[:, a:a + n] for a, n in MW.values())
        conv_sb = sb("conv_sb", [128, TAPS, CONV], where=early)
        w_conv = sb("w_conv", [128, TAPS, CONV], where=early)
        w_outn = sb("w_outn", [128, 2, D], where=early)
        small_sb = sb("small_sb", [PT, 3, MH], where=early)
        a_exp = sb("a_exp", [PT, MH], where=early)
        d_ident = sb("d_ident", [PT, MH, PT], where=early)
        xn = sb("xn", [PT, NP, D], where=early)
        u_tap = [sb(f"u_tap{k}", [D, B, S], where=early) for k in range(TAPS)]
        b_t, c_t = sb("b_t", [DS, TOK], where=early), sb("c_t", [DS, TOK], where=early)
        z_s = sb("z_s", [D, MH, TOK], where=early)
        x_s = sb("x_s", [PT, NP, DI], where=early)
        diag = sb("diag", [PT, NP, MH, PT], where=early)
        decay = sb("decay", [PT, NP * MH, PT], where=early)
        m_t = sb("m_t", [PT, NP, MH, PT], where=early)
        yg = sb("yg", [D, MH, TOK], where=early)
        sq = z_s
        dt_v, dt_e, dt_d, dt_z, dt_w, dt_q, dt_s, d_a = (
            sb(f"dt{i}", [PT, NP, MH], where=early) for i in range(8))
        early.close()

        k_stack[1] = sb("k_stack1", [STK, NG, CTX], F32R, cross)
        v_sb[1] = sb("v1", [CK, NC, VC], where=cross)
        q_stack = [sb(f"q_stack{i}", [STK, HQ], F32R, cross) for i in range(2)]
        q_all = sb("q_all", [D, TOK], F32R, cross)
        q_blk = [sb(f"q_blk{i}", [D, HQ], F32R, cross) for i in range(2)]
        q_parts = sb("q_parts", [3 * GR, NG, TOK], F32R, cross)
        part_max, row_max = sb("part_max", [128, NT, NKB], where=cross), sb("row_max", [128, NT], where=cross)
        neg_max = sb("neg_max", [128, NT], F32R, cross)
        inv = sb("inv", [128, 2, S], where=cross)
        u_mask, u_col = sb("u_mask", [128, PVC], where=cross), sb("u_col", [128, 2, S], where=cross)
        xn2, u2 = sb("xn2", [PT, NP, D], where=query), sb("u2", [D, TOK], where=query)
        q_f = [sb(f"q_f{i}", [3 * GR, TOK], where=query) for i in range(2)]
        query.close()
        p_sb = [sb(f"p{i}", [CK, HQ], where=cross) for i in range(3)]
        kept_rows = sb("kept_rows", [128, NT, CTX], U8, cross)
        kept_scores, masked_prob = sb("kept_scores", [128, KB], where=cross), sb("masked_prob", [128, HQ], where=cross)
        cross.close()
        context.close()

        xn3, sq3, rn3 = (sb(f"ffn{i}", [PT, NP, D], where=late) for i in range(3))
        f_t, fq_t, fk_t, r2_t = (sb(f"ffn_t{i}", [D, TOK], where=late) for i in range(4))
        fv = sb("fv", [128, NP, 2, VC], where=late)
        fqb = [sb(f"fqb{i}", [D, HQ], where=late) for i in range(B)]
        fk_hi = sb("fk_hi", [D, TOK], F32R, late)
        fqb_hi = [sb(f"fqb_hi{i}", [D, HQ], F32R, late) for i in range(4)]
        f_max = sb("f_max", [128, NP, NT, 2], where=late)
        f_neg = sb("f_neg", [128, NP, NT, 2], F32R, late)
        f_row = [sb(f"f_row{i}", [2, HQ], F32R, late) for i in range(2)]
        fp = [sb(f"fp{i}", [128, HQ], where=late) for i in range(2)]
        fu, fc = sb("fu", [128, 2, PVC], where=late), sb("fc", [128, 2, 2, S], where=late)
        f_inv = sb("f_inv", [128, 2, 2, S], where=late)
        h_t = [sb(f"h_t{i}", [128, NF, TOK], where=late) for i in range(2)]
        silu_a = [sb(f"silu_a{i}", [128, HALF], where=late) for i in range(2)]
        logits, top = sb("logits", [PT, NP, NE], where=late), sb("top", [PT, NP, 8], where=late)
        top_i, top_f = sb("top_i", [PT, NP, 8], U32, late), sb("top_f", [PT, NP, 2], where=late)
        gap2, e2, den2, r_1, r_2 = (sb(f"gate{i}", [PT, NP], where=late) for i in range(5))
        g_1, g_2, gates = (sb(f"gates{i}", [PT, NP, NE], where=late) for i in range(3))
        acc = sb("acc", [PT, NP, D], where=late)
        late.close()

        ld_x, ld_c, ld_w, ld_m, ld_s, ld_f = (sem(n) for n in ("ld_x", "ld_c", "ld_w", "ld_m", "ld_s", "ld_f"))
        ctx_in = [sem(f"ctx_in{i}") for i in range(2)]
        stacked = [sem(f"stacked{i}") for i in range(2)]
        k_ps, k_hi_done, k_lo_done = sem("k_ps"), sem("k_hi_done"), sem("k_lo_done")
        v_ps, v_done = sem("v_ps"), sem("v_done")
        q_blk_done, q_stack_done = sem("q_blk_done"), sem("q_stack_done")
        mx_ps, mx_read = sem("mx_ps"), sem("mx_read")
        max_done, neg_done = sem("max_done"), sem("neg_done")
        row_ps, row_done = sem("row_ps"), sem("row_done")
        st_ps, exp_done, pv_done = sem("st_ps"), sem("exp_done"), sem("pv_done")
        masked_done, half_fold, fold_done = sem("masked_done"), sem("half_fold"), sem("fold_done")
        den_ps, inv_done, o_done = sem("den_ps"), sem("inv_done"), sem("o_done")
        sig = {n: sem(n) for n in """
            fk_hi fq_hi const v_const stats_done aggr rstd_done xn u_ps u_mid tap dt_ps dt_in dt_abs dt_exp dt_scaled
            da_exp diag z_ps z_done bc_ps bc_done xc_ps x_done g_ps decay_ps decay m_half m_done y_ps yg sq
            o_ps ss_ps w_conv w_outn a_exp d_ident x1 u2_ps u2 q_ps q_f q_hi q_lo qa_ps qa bq
            x2_ps bv ss_done rn f_ps f_t fq_ps fq fk fv_ps fv fqb_even fqb_odd fmx_ps f_max f_neg frow_ps frow
            fst_ps fexp fpv_ps fu ffold_half ffold fden_ps f_inv fo fo_ps h1 r2_ps r2 lg_ps gap gexp gates
            ab_ps silu hid w2_ps w2_read fv_const""".split()}
        ld_k, any_done, flag_ps, flag_done = sem("ld_k"), sem("any_done"), sem("flag_ps"), sem("flag_done")
        raw_in, kept_done, part_done = sem("raw_in"), sem("kept_done"), sem("part_done")
        raw_exp, neg_spread, masked_prob_done = sem("raw_exp"), sem("neg_spread"), sem("masked_prob_done")

        def steps(eng, name):
            s, n = sem(name), [0]

            def step(ins):
                ins.then_inc(s, 1)
                n[0] += 1
                eng.wait_ge(s, n[0])
            return step

        def col(t, j):
            return t[:, j:j + 1]

        def bc(ap, shape, *at):
            for i in at:
                ap = ap.unsqueeze(i)
            return ap.broadcast_to(shape)

        flat_tap = [t[:, :, :].rearrange("p b s -> p (b s)") for t in u_tap]
        halves = [slice(0, HALF), slice(HALF, TOK)]

        def split(ap):
            return ap.rearrange("p (h n) -> p h n", h=2)

        block = es.enter_context(nc.Block())

        def pipeline(eng, iteration):
            iteration(Batch(None, 0))
            with eng.Fori(0, 6) as r:
                iteration(Batch(r, 1))
                iteration(Batch(r, 2))
            for k in range(13, B + 1):
                iteration(Batch(None, k))

        def by_mask(eng, cross_attention):
            eng.wait_ge(flag_done, 1)
            with eng.If(eng.value_load(flag[0:1, 0:1]) > 0):
                cross_attention(True)
            with eng.Else():
                cross_attention(False)

        def keys_read(b):
            return b.plus(1).count(NKB) if b.within(B) else B * NKB

        def fo_view(j, a):
            return o_all[:, a, j * PT:(j + 1) * PT]

        def units_of_step(s):
            return range(3) if s == 0 else range(2 * s + 1, min(2 * s + 3, NU))

        @block.sync
        def _(sp):
            tok = "(j p) d -> p j d"
            sp.dma_start(x_sb[:, :, :], x.rearrange(tok, p=PT)).then_inc(ld_x, 16)
            sp.dma_start(cst[:, :], cst_d).then_inc(ld_c, 16)
            sp.dma_start(key_mask[:, :, :], mask_t).then_inc(ld_k, 16)
            sp.dma_start(mw[:, :], mw_d).then_inc(ld_m, 16)

            def load_ctx(b):
                wait(sp, v_ps, b.plus(-1).count(NKB))
                sp.dma_start(ctx_sb[b.parity][:, :], ctx_t[:, bass.ds(b.count(CTX), CTX)]).then_inc(ctx_in[b.parity], 16)

            def stack_keys(b):
                split_done, used = in_register(sp, b.plus(1).count(NKB)), in_register(sp, b.plus(-1).count(NC))
                wait(sp, k_lo_done, split_done)
                wait(sp, st_ps, used)
                p = b.parity
                for n, part in enumerate((k_hi, k_lo, k_hi)):
                    for q in range(NG):
                        sp.dma_start(k_stack[p][n * GR:(n + 1) * GR, q, :].bitcast(F32),
                                     part[p][q * GR:(q + 1) * GR, :].bitcast(F32)).then_inc(stacked[p], 16)

            sp.dma_start(conv_sb[:, :, :], conv_w.unsqueeze(0).broadcast_to([128, TAPS, CONV])).then_inc(ld_s, 16)
            sp.dma_start(small_sb[:, :, :], small.unsqueeze(0).broadcast_to([PT, 3, MH])).then_inc(ld_s, 16)
            sp.dma_start(row_sb[:, :], rows).then_inc(ld_s, 16)
            sp.dma_start(xw[:, :], xw_d).then_inc(ld_w, 16)
            load_ctx(Batch(None, 0))
            load_ctx(Batch(None, 1))
            sp.dma_start(fw[:, :], fw_d).then_inc(ld_f, 16)
            stack_keys(Batch(None, 0))
            load_ctx(Batch(None, 2))
            wait(sp, sig["x1"], NP)
            stack_keys(Batch(None, 1))

            def iteration(i):
                if i.plus(3).within(B):
                    load_ctx(i.plus(3))
                if i.plus(2).within(B):
                    stack_keys(i.plus(2))

            pipeline(sp, iteration)
            wait(sp, sig["w2_read"], NP * NE)
            sp.dma_start(out.rearrange(tok, p=PT), acc[:, :, :]).then_inc(ld_x, 16)
            sp.wait_ge(ld_x, 32)

        @block.tensor
        def _(pe):
            def mm(o, lhs, rhs, start=True, stop=True):
                return pe.matmul(o, lhs, rhs, start=start, stop=stop, skip_group_check=True)

            def key_product(b, n):
                if n == 0:
                    wait(pe, ctx_in[b.parity], b.buffer_count(16))
                    if b.reg is None and b.k == 1:
                        wait(pe, v_done, NKB)
                    elif b.reg is not None or b.k > 1:
                        wait(pe, row_done, b.plus(-1).count(2))
                else:
                    wait(pe, k_lo_done, b.count(NKB, n))
                mm(ms[:, 0:KB], wk_t, ctx_sb[b.parity][:, n * KB:(n + 1) * KB]).then_inc(k_ps, 1)

            def value_product(b, n):
                if n == 0:
                    if b.reg is None and b.k == 0:
                        wait(pe, k_lo_done, NKB)
                    else:
                        wait(pe, k_lo_done, keys_read(b.plus(1)))
                        wait(pe, inv_done, b.plus(-1).count(1))
                else:
                    wait(pe, v_done, b.count(NKB, n))
                for c in range(4):
                    s = (4 * n + c) * CK
                    last = mm(ms[0:CK, c * D:(c + 1) * D], ctx_sb[b.parity][:, s:s + CK], wv_t)
                last.then_inc(v_ps, 1)

            def max_product(b, u):
                t, k = divmod(u, NKB)
                if u == 0:
                    wait(pe, q_blk_done, b.plus(1).count(1))
                    wait(pe, k_hi_done, b.plus(1).count(NKB))
                wait(pe, mx_read, b.count(NU, u - 1))
                mm(mx[(NU * b.parity + u) % 2][:, 0:KB], q_blk[b.parity][:, t * 128:(t + 1) * 128],
                   k_hi[b.parity][:, k * KB:(k + 1) * KB]).then_inc(mx_ps, 1)

            def row_product(b, n):
                wait(pe, neg_done, b.count(2, n + 1))
                if n == 1:
                    wait(pe, row_done, b.count(2, 1))
                elif b.reg is None and b.k == 0:
                    wait(pe, k_lo_done, 2 * NKB)
                else:
                    wait(pe, v_done, b.plus(1).count(NKB))
                ts = range(4) if n == 0 else range(4, NT)
                for t in ts:
                    last = mm(ms[0:1, (t - ts[0]) * 128:(t - ts[0] + 1) * 128], col(neg_max, t), ident_r[:, :])
                last.then_inc(row_ps, 1)

            def score_product(b, s):
                p = b.parity
                if s == 0:
                    wait(pe, stacked[p], b.buffer_count(16 * 3 * NG))
                    wait(pe, q_stack_done, b.plus(1).count(1))
                    wait(pe, row_done, b.plus(1).count(2))
                wait(pe, exp_done, b.count(NC, s - 1))
                for q in range(NG):
                    last = mm(st[s % 2][0:CK, q // 2, (q % 2) * GQ:(q % 2 + 1) * GQ],
                              k_stack[p][:, q, s * CK:(s + 1) * CK], q_stack[p][:, q * GQ:(q + 1) * GQ])
                last.then_inc(st_ps, 1)

            def pv_product(b, s):
                wait(pe, exp_done, b.count(NC, s + 1))
                if s == 0:
                    wait(pe, masked_done, b.count(2))
                    wait(pe, v_done, b.plus(1).count(NKB))
                for t, vc, qc, heads, oc in VGROUPS:
                    last = mm(pv[32 * t:32 * t + 32, oc:oc + heads * S], v_sb[b.parity][:, s, vc:vc + 32],
                              p_sb[s % 3][:, qc:qc + heads * S], start=(s == 0 and oc == 0), stop=(s == NC - 1))
                last.then_inc(pv_done, 1)

            def den_product(b):
                wait(pe, fold_done, b.plus(1).count(1))
                wait(pe, k_lo_done, keys_read(b.plus(3)))
                wait(pe, inv_done, b.count(1))
                mm(ms[:, 0:2 * S], spread, u_col[:, :, :].rearrange("p a q -> p (a q)")).then_inc(den_ps, 1)

            def iteration(i):
                for s in range(NC):
                    units = units_of_step(s) if i.plus(1).within(B) else ()
                    if s == ROW_STEPS[1] and i.plus(1).within(B):
                        row_product(i.plus(1), 1)
                    if i.within(B):
                        score_product(i, s)
                    for u in units[:2]:
                        max_product(i.plus(1), u)
                    if s < NKB and i.plus(2).within(B):
                        key_product(i.plus(2), s)
                    for u in units[2:]:
                        max_product(i.plus(1), u)
                    if s == 3 and i.plus(-1).within(B):
                        den_product(i.plus(-1))
                    if 5 <= s < 5 + NKB and i.plus(1).within(B):
                        value_product(i.plus(1), s - 5)
                    if s == ROW_STEPS[0] and i.plus(1).within(B):
                        row_product(i.plus(1), 0)
                    if s == 0 and i.plus(-1).within(B):
                        pv_product(i.plus(-1), NC - 1)
                    elif s > 0 and i.within(B):
                        pv_product(i, s - 1)

            b0, b1 = Batch(None, 0), Batch(None, 1)
            pe.wait_ge(ld_c, 16)
            pe.wait_ge(sig["xn"], NP)
            for j in range(NP):
                last = pe.transpose(st[0][:, j // 4, (j % 4) * PT:(j % 4 + 1) * PT], xn[:, j, :], ident[0:PT, 0:PT])
            last.then_inc(sig["u_ps"], 1)
            pe.wait_ge(any_done, 1)
            mm(pv[0:1, 0:1], any_masked[:, :], ones[0:CK, 0:1]).then_inc(flag_ps, 1)
            pe.wait_ge(ld_w, 16)
            key_product(b0, 0)
            pe.wait_ge(sig["u_mid"], 1)
            pe.wait_ge(ld_m, 16)
            for j in range(NP):
                last = mm(mx[0][0:PT, MH * j:MH * (j + 1)], flat_tap[3][:, j * PT:(j + 1) * PT],
                          w_in[:, 2 * DI + 2 * DS:])
            last.then_inc(sig["dt_ps"], 1)
            for c in range(MH):
                for h in range(2):
                    last = mm(st[c][:, h, 0:HALF], w_in[:, c * 128:(c + 1) * 128], flat_tap[3][:, halves[h]])
                last.then_inc(sig["z_ps"], 1)
            key_product(b0, 1)
            pe.wait_ge(sig["w_conv"], 1)
            pe.wait_ge(sig["tap"], TAPS - 1)
            for h in (1, 0):
                if h == 0:
                    pe.wait_ge(sig["dt_in"], 1)
                for k in range(TAPS):
                    last = mm(mx[h][:, 0:HALF], w_conv[:, k, DI:CONV], flat_tap[k][:, halves[h]],
                              start=(k == 0), stop=(k == TAPS - 1))
                last.then_inc(sig["bc_ps"], 1)
            key_product(b0, 2)
            pe.wait_ge(sig["bc_done"], 4)
            for j in range(NP):
                t = slice(j * PT, (j + 1) * PT)
                last = mm(mx[j // 4][0:PT, (j % 4) * PT:(j % 4 + 1) * PT], b_t[:, t], c_t[:, t])
            last.then_inc(sig["g_ps"], 1)
            pe.wait_ge(sig["diag"], 1)
            pe.wait_ge(sig["z_done"], 2)
            for n in range(4):
                mm(st[n // 2][0:PT, n % 2, 0:HALF], ones[0:PT, 0:PT],
                   diag[:, 2 * n:2 * n + 2, :, :].rearrange("p j h t -> p (j h t)")).then_inc(sig["decay_ps"], 1)
            pe.wait_ge(ld_s, 48)
            for j in range(NP):
                if j % 2 == 0:
                    pe.wait_ge(sig["decay"], 4 * (j // 2 + 1))
                o = st[j // 4][0:PT, (j // 2) % 2, (j % 2) * DI:(j % 2 + 1) * DI]
                mm(o, ones[0:1, 0:PT], row_sb[:, 0:DI], stop=False)
                for k in range(TAPS):
                    last = mm(o, flat_tap[k][:, j * PT:(j + 1) * PT], w_conv[:, k, 0:DI],
                              start=False, stop=(k == TAPS - 1))
                if j % 4 == 3:
                    last.then_inc(sig["xc_ps"], 1)
                if j in (1, 3, 5):
                    value_product(b0, j // 2)
            pe.wait_ge(sig["m_done"], 1)
            pe.wait_ge(sig["x_done"], 2)
            for h in range(MH):
                for j in range(NP):
                    last = mm(st[h][:, j // 4, (j % 4) * PT:(j % 4 + 1) * PT], x_s[:, j, h * HD:(h + 1) * HD],
                              m_t[:, j, h, :])
                last.then_inc(sig["y_ps"], 1)
            pe.wait_ge(sig["yg"], 2)
            pe.wait_ge(sig["w_outn"], 2)
            for j in range(NP):
                for h in range(MH):
                    last = mm(mx[j // 4][0:PT, (j % 4) * D:(j % 4 + 1) * D], yg[:, h, j * PT:(j + 1) * PT],
                              w_outn[:, h, :], start=(h == 0), stop=(h == 1))
            last.then_inc(sig["o_ps"], 1)
            pe.wait_ge(sig["sq"], 1)
            for j in range(NP):
                for h in range(MH):
                    last = mm(pv[0:PT, j:j + 1], sq[:, h, j * PT:(j + 1) * PT], ones[:, 0:1],
                              start=(h == 0), stop=(h == 1))
            last.then_inc(sig["ss_ps"], 1)

            key_product(b1, 0)
            pe.wait_ge(sig["xn"], 2 * NP)
            for j in range(NP):
                last = pe.transpose(st[0][:, j // 4, (j % 4) * PT:(j % 4 + 1) * PT], xn2[:, j, :], ident[0:PT, 0:PT])
            last.then_inc(sig["u2_ps"], 1)
            key_product(b1, 1)
            pe.wait_ge(sig["u2"], 1)
            for h in range(2):
                last = mm(mx[h][:, 0:HALF], wq_t, u2[:, halves[h]])
            last.then_inc(sig["qa_ps"], 1)
            key_product(b1, 2)
            for q in range(NG):
                if q == 2:
                    pe.wait_ge(sig["qa"], 2)
                    for u in range(2):
                        max_product(b0, u)
                wait(pe, sig["q_f"], q - 1)
                for h in range(2):
                    last = mm(st[(q + 1) % 2][0:3 * GR, h, 0:HALF], wq3[:, q * 3 * GR:(q + 1) * 3 * GR],
                              u2[:, halves[h]])
                last.then_inc(sig["q_ps"], 1)
            for u in range(2, NU):
                max_product(b0, u)
            for n in range(2):
                row_product(b0, n)

            pipeline(pe, iteration)

            pe.wait_ge(sig["bv"], 2)
            for j in range(NP):
                o = mx[j // 4][0:PT, (j % 4) * D:(j % 4 + 1) * D]
                mm(o, ones[0:1, 0:PT], row_sb[:, DI:DI + D], stop=False)
                for a in range(2):
                    last = mm(o, o_all[:, a, j * PT:(j + 1) * PT], wo_rows[:, a * D:(a + 1) * D],
                              start=False, stop=(a == 1))
                if j % 4 == 3:
                    last.then_inc(sig["x2_ps"], 1)

            def transposed(src, out_sig):
                for j in range(NP):
                    last = pe.transpose(st[0][:, j // 4, (j % 4) * PT:(j % 4 + 1) * PT], src[:, j, :],
                                        ident[0:PT, 0:PT])
                last.then_inc(out_sig, 1)

            pe.wait_ge(sig["rn"], 1)
            transposed(rn3, sig["f_ps"])
            pe.wait_ge(sig["f_t"], 1)
            pe.wait_ge(ld_f, 16)
            for c, wgt in ((1, fwq), (0, fwk)):
                for h in range(2):
                    last = mm(st[c][:, h, 0:HALF], wgt, f_t[:, halves[h]])
                last.then_inc(sig["fq_ps"], 1)
            for j in range(NP):
                for a in range(2):
                    s = (2 * j + a) * S
                    last = mm(mx[j // 4][64 * a:64 * a + S, (j % 4) * D:(j % 4 + 1) * D], f_t[:, s:s + S], fwv)
            last.then_inc(sig["fv_ps"], 1)

            def self_max(j):
                if j == 0:
                    pe.wait_ge(sig["fk_hi"], 1)
                    pe.wait_ge(sig["fv"], 4)
                for a in range(2):
                    pe.wait_ge(sig["fq_hi"], 2 * j + a + 1)
                    wait(pe, sig["f_max"], 2 * j + a - 1)
                    for t in range(NT):
                        last = mm(mx[a][:, t * S:(t + 1) * S], fqb_hi[2 * (j % 2) + a][:, t * 128:(t + 1) * 128],
                                  fk_hi[:, (2 * j + a) * S:(2 * j + a + 1) * S])
                    last.then_inc(sig["fmx_ps"], 1)

            def self_row(j, n):
                if n == 0:
                    pe.wait_ge(sig["f_neg"], j + 1)
                    if j == 0:
                        pe.wait_ge(sig["f_max"], 2 * NP)
                wait(pe, sig["frow"], 2 * j + n)
                ts = range(4) if n == 0 else range(4, NT)
                for t in ts:
                    last = mm(mx[0][0:2, (t - ts[0]) * 128:(t - ts[0] + 1) * 128], f_neg[:, j, t, :], ident_r[:, :])
                last.then_inc(sig["frow_ps"], 1)

            def self_scores(j, h):
                if h == 0:
                    wait(pe, sig["fexp"], j - 1)
                pe.wait_ge(sig["frow"], 2 * j + h + 1)
                o = st[j % 2][:, h, 0:HALF]
                mm(o, half_r[:, :], f_row[j % 2][:, halves[h]], stop=False)
                for a in range(2):
                    last = mm(o[64 * a:64 * a + S], fk_t[:, (2 * j + a) * S:(2 * j + a + 1) * S],
                              fqb[2 * j + a][:, halves[h]], start=False)
                if h == 1:
                    last.then_inc(sig["fst_ps"], 1)

            def self_values(j):
                pe.wait_ge(sig["fexp"], j + 1)
                wait(pe, sig["fu"], 4 * j)
                for a, bank in enumerate((pv, ms)):
                    for t, vc, qc, heads, oc in VGROUPS:
                        last = mm(bank[32 * t:32 * t + 32, oc:oc + heads * S], fv[:, j, a, vc:vc + 32],
                                  fp[j % 2][:, qc:qc + heads * S], start=(oc == 0))
                last.then_inc(sig["fpv_ps"], 1)

            def self_den(j):
                pe.wait_ge(sig["ffold"], j + 1)
                wait(pe, sig["f_inv"], j)
                mm(mx[1][:, 0:4 * S], spread, fc[:, :, :, :].rearrange("p a b q -> p (a b q)")) \
                    .then_inc(sig["fden_ps"], 1)

            for j in range(NP):
                self_max(j)
            pe.wait_ge(sig["fk"], 1)
            for n in range(2):
                self_row(0, n)
            for j in range(NP + 2):
                for h in range(2):
                    if j + 1 < NP:
                        self_row(j + 1, h)
                    if j < NP:
                        self_scores(j, h)
                if j >= 2:
                    self_den(j - 2)
                if 1 <= j <= NP:
                    self_values(j - 1)
            pe.wait_ge(sig["fo"], NP)
            for j in range(NP):
                for a in range(2):
                    last = mm(mx[j // 4][0:PT, (j % 4) * D:(j % 4 + 1) * D], fo_view(j, a), fwo[:, a * D:(a + 1) * D],
                              start=(a == 0), stop=(a == 1))
                if j % 4 == 3:
                    last.then_inc(sig["fo_ps"], 1)

            pe.wait_ge(sig["rn"], 2)
            transposed(rn3, sig["r2_ps"])
            pe.wait_ge(sig["r2"], 1)
            for j in range(NP):
                last = mm(ms[0:PT, j * NE:(j + 1) * NE], r2_t[:, j * PT:(j + 1) * PT], gate_t)
            last.then_inc(sig["lg_ps"], 1)

            out_banks = [mx[0], mx[1], pv, ms]

            def expert_in(e, n):
                c, h = divmod(n, 2)
                g = 4 * e + n
                wait(pe, sig["hid"], g - 1)
                for a, wgt in enumerate((w1_t, w3_t)):
                    last = mm(st[g % 2][:, a, 0:HALF], wgt[:, e * FI + c * 128:e * FI + (c + 1) * 128],
                              r2_t[:, halves[h]])
                last.then_inc(sig["ab_ps"], 1)

            def expert_out(e, q):
                bank = out_banks[(2 * e + q) % 4]
                pe.wait_ge(sig["hid"], 4 * e + 4)
                wait(pe, sig["w2_read"], NP * (e - 2) + 4 * q + 4)
                for j in range(4 * q, 4 * q + 4):
                    for c in range(NF):
                        last = mm(bank[0:PT, (j % 4) * D:(j % 4 + 1) * D], h_t[e % 2][:, c, j * PT:(j + 1) * PT],
                                  w2_t[:, (e * NF + c) * D:(e * NF + c + 1) * D], start=(c == 0), stop=(c == 1))
                last.then_inc(sig["w2_ps"], 1)

            pe.wait_ge(sig["gates"], 1)
            for e in range(NE + 1):
                for n in range(4):
                    if e < NE:
                        expert_in(e, n)
                    if e > 0 and n % 2 == 0:
                        expert_out(e - 1, n // 2)

        @block.vector
        def _(dv):
            step = steps(dv, "dve_step")
            norms = [0]

            def layer_norm(t, normed, which, meanwhile=None):
                norms[0] += 1
                for j in range(NP):
                    dv.bn_stats(stats[:, j, :], t[:, j, :]).then_inc(sig["stats_done"], 1)
                dv.wait_ge(sig["stats_done"], NP * norms[0])
                for j in range(NP):
                    dv.bn_aggr(mv[:, j, :], stats[:, j, :]).then_inc(sig["aggr"], 1)
                if meanwhile:
                    meanwhile()
                dv.wait_ge(sig["aggr"], NP * norms[0])
                dv.wait_ge(sig["rstd_done"], which)
                for j in range(NP):
                    dv.tensor_scalar(normed[:, j, :], t[:, j, :], mv[:, j, 0:1], rstd[:, j:j + 1], ALU.subtract,
                                     ALU.mult).then_inc(sig["xn"], 1)

            dv.memset(ones[:, :], 1.0).then_inc(sig["const"], 1)
            dv.memset(eps_col[:, :], EPS).then_inc(sig["const"], 1)
            step(dv.memset(masked_col[:, :], MASKED))
            for k in range(TAPS - 1):
                step(dv.memset(u_tap[k][:, :, 0:TAPS - 1 - k], 0.0))

            def key_low(b, n):
                c = slice(n * KB, (n + 1) * KB)
                wait(dv, k_hi_done, b.count(NKB, n + 1))
                dv.scalar_tensor_tensor(out=k_lo[b.parity][:, c], in0=ms[:, 0:KB], scalar=bk_col,
                                        in1=k_hi[b.parity][:, c].bitcast(F32), op0=ALU.add,
                                        op1=ALU.subtract).then_inc(k_lo_done, 1)

            dv.wait_ge(ld_x, 16)
            layer_norm(x_sb, xn, 1)
            dv.wait_ge(ld_k, 16)
            step(dv.tensor_scalar(key_masked[:, :, :], key_mask[:, :, :], 0, None, ALU.is_equal))
            dv.tensor_reduce(any_masked[:, :], key_masked[:, :, :].rearrange("p c q -> p (c q)"), AX, ALU.max) \
                .then_inc(any_done, 1)
            dv.wait_ge(ld_c, 16)
            dv.tensor_copy(ident_r[:, :], ident).then_inc(sig["const"], 1)
            dv.tensor_copy(half_r[:, :], half_rows[0:2]).then_inc(sig["const"], 1)
            dv.wait_ge(ld_w, 16)
            dv.tensor_scalar(bq_s[:, :], xw[:, XW["bq3"][0]:XW["bq3"][0] + NG + 1], SCALE, None,
                             ALU.mult).then_inc(sig["bq"], 1)

            dv.wait_ge(sig["u_ps"], 1)
            dv.tensor_copy(split(flat_tap[3]), st[0][:, :, 0:HALF]).then_inc(sig["u_mid"], 1)
            dv.wait_ge(sig["u_mid"], 1)
            for k in (2, 1, 0):
                d = TAPS - 1 - k
                dv.tensor_copy(u_tap[k][:, :, d:S], u_tap[3][:, :, 0:S - d]).then_inc(sig["tap"], 1)
            key_low(Batch(None, 0), 0)
            dv.wait_ge(flag_ps, 1)
            dv.tensor_copy(flag[:, :], pv[0:1, 0:1]).then_inc(flag_done, 1)
            dv.wait_ge(sig["dt_ps"], 1)
            dv.wait_ge(ld_s, 48)
            dv.tensor_tensor(dt_v[:, :, :], mx[0][0:PT, 0:NP * MH].rearrange("p (j h) -> p j h", h=MH),
                             bc(small_sb[:, 1, :], [PT, NP, MH], 1), ALU.add).then_inc(sig["dt_in"], 1)
            dv.wait_ge(sig["dt_in"], 1)
            dv.scalar_tensor_tensor(out=dt_d[:, :, :], in0=dt_v[:, :, :], scalar=-1.0, in1=dt_v[:, :, :],
                                    op0=ALU.mult, op1=ALU.max).then_inc(sig["dt_abs"], 1)
            dv.wait_ge(sig["dt_exp"], 1)
            step(dv.tensor_scalar(dt_z[:, :, :], dt_e[:, :, :], 2.0, None, ALU.add))
            step(dv.reciprocal(dt_z[:, :, :], dt_z[:, :, :]))
            step(dv.tensor_tensor(dt_z[:, :, :], dt_z[:, :, :], dt_e[:, :, :], ALU.mult))
            step(dv.tensor_tensor(dt_w[:, :, :], dt_z[:, :, :], dt_z[:, :, :], ALU.mult))
            step(dv.tensor_scalar(dt_q[:, :, :], dt_w[:, :, :], 1.0 / 17, None, ALU.mult))
            for k in range(15, 2, -2):
                step(dv.scalar_tensor_tensor(out=dt_q[:, :, :], in0=dt_q[:, :, :], scalar=1.0 / k,
                                             in1=dt_w[:, :, :], op0=ALU.add, op1=ALU.mult))
            step(dv.scalar_tensor_tensor(out=dt_q[:, :, :], in0=dt_q[:, :, :], scalar=1.0, in1=dt_z[:, :, :],
                                         op0=ALU.add, op1=ALU.mult))
            step(dv.tensor_scalar(dt_w[:, :, :], dt_v[:, :, :], 0.0, None, ALU.max))
            step(dv.scalar_tensor_tensor(out=dt_s[:, :, :], in0=dt_q[:, :, :], scalar=2.0, in1=dt_w[:, :, :],
                                         op0=ALU.mult, op1=ALU.add))
            dv.wait_ge(sig["a_exp"], 1)
            dv.tensor_tensor(dt_d[:, :, :], dt_s[:, :, :], bc(a_exp[:, :], [PT, NP, MH], 1), ALU.mult) \
                .then_inc(sig["dt_scaled"], 1)
            dv.wait_ge(sig["da_exp"], 1)
            dv.tensor_tensor(diag[:, :, :, :], bc(d_a[:, :, :], [PT, NP, MH, PT], 3),
                             bc(start_ident[0:PT], [PT, NP, MH, PT], 1, 1), ALU.mult).then_inc(sig["diag"], 1)
            key_low(Batch(None, 0), 1)
            key_low(Batch(None, 0), 2)
            for n in range(4):
                dv.wait_ge(sig["decay_ps"], n + 1)
                for k in range(4):
                    dv.tensor_tensor_scan(decay[:, 4 * n + k, :], st[n // 2][0:PT, n % 2, k * PT:(k + 1) * PT],
                                          ident[0:PT, 0:PT], 0.0, ALU.mult, ALU.add).then_inc(sig["decay"], 1)
            dv.wait_ge(sig["g_ps"], 1)
            dv.wait_ge(sig["decay"], NP * MH)
            for j in range(NP):
                for h in range(MH):
                    dv.scalar_tensor_tensor(out=m_t[:, j, h, :], in0=decay[:, MH * j + h, :], scalar=dt_s[:, j, h:h + 1],
                                            in1=mx[j // 4][0:PT, (j % 4) * PT:(j % 4 + 1) * PT], op0=ALU.mult,
                                            op1=ALU.mult).then_inc(sig["m_half"], 1)
            dv.wait_ge(sig["m_half"], NP * MH)
            dv.wait_ge(sig["d_ident"], 2)
            dv.tensor_tensor(m_t[:, :, :, :], m_t[:, :, :, :], bc(d_ident[:, :, :], [PT, NP, MH, PT], 1), ALU.add) \
                .then_inc(sig["m_done"], 1)
            dv.wait_ge(sig["z_done"], 2)
            for h in range(MH):
                dv.wait_ge(sig["y_ps"], h + 1)
                dv.tensor_tensor(split(yg[:, h, :]), st[h][:, :, 0:HALF], split(z_s[:, h, :]), ALU.mult) \
                    .then_inc(sig["yg"], 1)
            dv.wait_ge(sig["o_ps"], 1)
            dv.wait_ge(sig["rstd_done"], 2)
            for j in range(NP):
                dv.scalar_tensor_tensor(out=x_sb[:, j, :], in0=mx[j // 4][0:PT, (j % 4) * D:(j % 4 + 1) * D],
                                        scalar=col(rstd, j), in1=x_sb[:, j, :], op0=ALU.mult,
                                        op1=ALU.add).then_inc(sig["x1"], 1)
            dv.wait_ge(sig["x1"], NP)

            layer_norm(x_sb, xn2, 3, lambda: key_low(Batch(None, 1), 0))
            dv.wait_ge(sig["u2_ps"], 1)
            dv.tensor_copy(split(u2[:, :]), st[0][:, :, 0:HALF]).then_inc(sig["u2"], 1)
            key_low(Batch(None, 1), 1)
            key_low(Batch(None, 1), 2)
            for q in range(NG):
                dv.wait_ge(sig["q_f"], q + 1)
                dv.tensor_copy(q_parts[:, q, :], q_f[q % 2][:, :]).then_inc(sig["q_hi"], 1)
                dv.wait_ge(sig["q_hi"], q + 1)
                lo = slice(2 * GR, 3 * GR)
                dv.tensor_tensor(q_parts[lo, q, :], q_f[q % 2][lo, :], q_parts[lo, q, :].bitcast(F32),
                                 ALU.subtract).then_inc(sig["q_lo"], 1)

            def read_max(b, u, masked):
                t, k = divmod(u, NKB)
                scores = mx[(NU * b.parity + u) % 2][:, 0:KB]
                part = part_max[:, t, k:k + 1]
                wait(dv, mx_ps, b.count(NU, u + 1))
                if not masked:
                    dv.tensor_reduce(part, scores, AX, ALU.max).then_inc(mx_read, 1)
                    return
                if b.reg is None and b.k == 0:
                    dv.wait_ge(kept_done, NU)
                wait(dv, part_done, b.count(NU, u))
                dv.scalar_tensor_tensor(out=kept_scores[:, :], in0=scores, scalar=-MASKED,
                                        in1=kept_rows[:, t, k * KB:(k + 1) * KB], op0=ALU.add,
                                        op1=ALU.mult).then_inc(mx_read, 1)
                wait(dv, mx_read, b.count(NU, u + 1))
                dv.tensor_reduce(part, kept_scores[:, :], AX, ALU.max).then_inc(part_done, 1)

            def negate_max(b, n, masked):
                t = slice(0, 4) if n == 0 else slice(4, NT)
                wait(dv, part_done if masked else mx_read, b.count(NU, NKB * t.stop))
                dv.tensor_reduce(row_max[:, t], part_max[:, t, :], AX, ALU.max).then_inc(max_done, 1)
                wait(dv, max_done, b.count(2, n + 1))
                dv.tensor_scalar(neg_max[:, t], row_max[:, t], -1.0, -MASKED if masked else None, ALU.mult,
                                 *([ALU.add] if masked else [])).then_inc(neg_done, 1)

            def mask_probs(b, s):
                exps, spreads = in_register(dv, b.count(NC, s + 1)), in_register(dv, b.plus(1).count(1))
                dv.wait_ge(flag_done, 1)
                dv.wait_ge(raw_exp, exps)
                if s == 0:
                    dv.wait_ge(masked_prob_done, spreads)
                dv.copy_predicated(p_sb[s % 3][:, :].rearrange("p (h q) -> p h q", h=H),
                                   bc(key_masked[:, s, :], [CK, H, S], 1),
                                   masked_prob[0:CK, :].rearrange("p (h q) -> p h q", h=H)) \
                    .then_inc(exp_done, 1)

            def mask_values(b):
                wait(dv, pv_done, b.plus(1).count(NC))
                wait(dv, fold_done, b.count(1))
                for r, c in VALUE_PARTS:
                    dv.tensor_tensor(u_mask[r, c], pv[r, c], block_mask[r, c], ALU.mult).then_inc(masked_done, 1)

            def divide(b):
                wait(dv, den_ps, b.plus(1).count(1))
                dv.reciprocal(inv[:, :, :], ms[:, 0:2 * S].rearrange("p (a q) -> p a q", a=2)).then_inc(inv_done, 1)
                wait(dv, inv_done, b.plus(1).count(1))
                dv.tensor_tensor(o_all[:, :, bass.ds(b.count(S), S)], u_col[:, :, :], inv[:, :, :], ALU.mult) \
                    .then_inc(o_done, 1)

            def iteration(i, masked):
                if masked and i.plus(-1).within(B):
                    mask_probs(i.plus(-1), NC - 1)
                for s in range(NC):
                    if i.plus(1).within(B):
                        if s == 6:
                            negate_max(i.plus(1), 0, masked)
                        for u in units_of_step(s):
                            read_max(i.plus(1), u, masked)
                        if s == 10:
                            negate_max(i.plus(1), 1, masked)
                    if s < NKB and i.plus(2).within(B):
                        key_low(i.plus(2), s)
                    if s == 3 and i.plus(-1).within(B):
                        divide(i.plus(-1))
                    if s == 0 and i.plus(-1).within(B):
                        mask_values(i.plus(-1))
                    elif masked and s > 0 and i.within(B):
                        mask_probs(i, s - 1)

            def cross_attention(masked):
                for u in range(NU):
                    read_max(Batch(None, 0), u, masked)
                for n in range(2):
                    negate_max(Batch(None, 0), n, masked)
                pipeline(dv, lambda i: iteration(i, masked))

            by_mask(dv, cross_attention)

            dv.wait_ge(o_done, B)
            for a in range(2):
                dv.tensor_scalar(o_all[:, a, :], o_all[:, a, :], col(bv_rows, a), None, ALU.add) \
                    .then_inc(sig["bv"], 1)
            for c in range(2):
                dv.wait_ge(sig["x2_ps"], c + 1)
                step(dv.tensor_tensor(x_sb[:, 4 * c:4 * c + 4, :], x_sb[:, 4 * c:4 * c + 4, :],
                                      mx[c][0:PT, :].rearrange("p (j d) -> p j d", d=D), ALU.add))
            layer_norm(x_sb, xn3, 4)
            dv.wait_ge(sig["xn"], 3 * NP)

            def rms_norm(which):
                step(dv.tensor_tensor(sq3[:, :, :], xn3[:, :, :], xn3[:, :, :], ALU.mult))
                dv.tensor_reduce(ssum[:, :], sq3[:, :, :], AX, ALU.add).then_inc(sig["ss_done"], 1)
                dv.wait_ge(sig["rstd_done"], which)
                dv.tensor_tensor(rn3[:, :, :], xn3[:, :, :], bc(rstd[:, :], [PT, NP, D], 2), ALU.mult) \
                    .then_inc(sig["rn"], 1)

            rms_norm(5)
            dv.wait_ge(sig["fq_ps"], 2)
            dv.tensor_copy(split(fk_t[:, :]), st[0][:, :, 0:HALF]).then_inc(sig["fk"], 1)

            def odd_queries(j):
                if j == 0:
                    dv.wait_ge(sig["fq"], 1)
                dv.tensor_tensor(fqb[2 * j + 1][:, :].rearrange("p (h q) -> p h q", h=H),
                                 bc(fq_t[:, (2 * j + 1) * S:(2 * j + 2) * S], [D, H, S], 1),
                                 bc(head_mask, [D, H, S], 2), ALU.mult).then_inc(sig["fqb_odd"], 1)

            def self_max(j):
                for a in range(2):
                    dv.wait_ge(sig["fmx_ps"], 2 * j + a + 1)
                    dv.tensor_reduce(f_max[:, j, :, a], mx[a][:, 0:NT * S].rearrange("p (t k) -> p t k", k=S), AX,
                                     ALU.max).then_inc(sig["f_max"], 1)
                dv.wait_ge(sig["f_max"], 2 * j + 2)
                dv.tensor_scalar(f_neg[:, j, :, :], f_max[:, j, :, :], -1.0, None, ALU.mult).then_inc(sig["f_neg"], 1)

            def self_mask(j):
                dv.wait_ge(sig["fpv_ps"], j + 1)
                wait(dv, sig["ffold"], j)
                for a, bank in enumerate((pv, ms)):
                    for r, c in VALUE_PARTS:
                        dv.tensor_tensor(fu[r, a, c], bank[r, c], block_mask[r, c], ALU.mult).then_inc(sig["fu"], 1)

            def self_divide(j):
                dv.wait_ge(sig["fden_ps"], j + 1)
                dv.reciprocal(f_inv[:, :, :, :].rearrange("p a b q -> p (a b q)"), mx[1][:, 0:4 * S]) \
                    .then_inc(sig["f_inv"], 1)
                dv.wait_ge(sig["f_inv"], j + 1)
                dv.tensor_tensor(o_all[:, :, j * PT:(j + 1) * PT], fc[:, :, :, :].rearrange("p a b q -> p a (b q)"),
                                 f_inv[:, :, :, :].rearrange("p a b q -> p a (b q)"), ALU.mult) \
                    .then_inc(sig["fo"], 1)

            odd_queries(0)
            odd_queries(1)
            for j in range(NP):
                if j + 2 < NP:
                    odd_queries(j + 2)
                self_max(j)
            for j in range(NP + 1):
                if j >= 1:
                    self_divide(j - 1)
                if j < NP:
                    self_mask(j)

            for c in range(2):
                dv.wait_ge(sig["fo_ps"], c + 1)
                step(dv.tensor_tensor(xn3[:, 4 * c:4 * c + 4, :], xn3[:, 4 * c:4 * c + 4, :],
                                      mx[c][0:PT, :].rearrange("p (j d) -> p j d", d=D), ALU.add))
            rms_norm(6)
            step(dv.tensor_tensor(acc[:, :, :], xn3[:, :, :], x_sb[:, :, :], ALU.add))
            dv.wait_ge(sig["lg_ps"], 1)
            step(dv.tensor_copy(logits[:, :, :], ms[0:PT, 0:NP * NE].rearrange("p (j e) -> p j e", e=NE)))
            for j in range(NP):
                step(dv.max(top[:, j, :], logits[:, j, :]))
                step(dv.max_index(top_i[:, j, :], top[:, j, :], logits[:, j, :]))
            dv.tensor_tensor(gap2[:, :], top[:, :, 1], top[:, :, 0], ALU.subtract).then_inc(sig["gap"], 1)
            step(dv.tensor_copy(top_f[:, :, :], top_i[:, :, 0:2]))
            dv.wait_ge(sig["gexp"], 1)
            step(dv.tensor_scalar(den2[:, :], e2[:, :], 1.0, None, ALU.add))
            step(dv.reciprocal(r_1[:, :], den2[:, :]))
            step(dv.tensor_tensor(r_2[:, :], e2[:, :], r_1[:, :], ALU.mult))
            for k, (g, r) in enumerate(((g_1, r_1), (g_2, r_2))):
                step(dv.tensor_tensor(g[:, :, :], bc(expert_id[0:PT], [PT, NP, NE], 1),
                                      bc(top_f[:, :, k], [PT, NP, NE], 2), ALU.is_equal))
                step(dv.tensor_tensor(g[:, :, :], g[:, :, :], bc(r[:, :], [PT, NP, NE], 2), ALU.mult))
            dv.tensor_tensor(gates[:, :, :], g_1[:, :, :], g_2[:, :, :], ALU.add).then_inc(sig["gates"], 1)
            dv.wait_ge(sig["gates"], 1)

            def hidden(e, n):
                c, h = divmod(n, 2)
                g = 4 * e + n
                dv.wait_ge(sig["silu"], g + 1)
                wait(dv, sig["w2_ps"], 2 * (e - 1))
                dv.tensor_tensor(h_t[e % 2][:, c, halves[h]], silu_a[g % 2][:, :], st[g % 2][:, 1, 0:HALF],
                                 ALU.mult).then_inc(sig["hid"], 1)

            def add_expert(e, q):
                bank = [mx[0], mx[1], pv, ms][(2 * e + q) % 4]
                dv.wait_ge(sig["w2_ps"], 2 * e + q + 1)
                for j in range(4 * q, 4 * q + 4):
                    wait(dv, sig["w2_read"], NP * (e - 1) + j + 1)
                    dv.scalar_tensor_tensor(out=acc[:, j, :], in0=bank[0:PT, (j % 4) * D:(j % 4 + 1) * D],
                                            scalar=gates[:, j, e:e + 1], in1=acc[:, j, :], op0=ALU.mult,
                                            op1=ALU.add).then_inc(sig["w2_read"], 1)

            for e in range(NE + 1):
                for n in range(4):
                    if e < NE:
                        hidden(e, n)
                    if e > 0 and n % 2 == 0:
                        add_expert(e - 1, n // 2)

        @block.scalar
        def _(ac):
            step = steps(ac, "act_step")

            def rstd_of(src, scale):
                step(ac.activation(lnv[:, :], src, ACT.Ln, bias=eps_col[0:PT], scale=scale))
                ac.activation(rstd[:, :], lnv[:, :], ACT.Exp, scale=-0.5).then_inc(sig["rstd_done"], 1)

            def key_high(b, n):
                wait(ac, k_ps, b.count(NKB, n + 1))
                ac.activation(k_hi[b.parity][:, n * KB:(n + 1) * KB], ms[:, 0:KB], ACT.Identity, bias=bk_col) \
                    .then_inc(k_hi_done, 1)

            def take_values(b, n):
                wait(ac, v_ps, b.count(NKB, n + 1))
                dst = v_sb[b.parity][:, 4 * n:4 * n + 4, 0:VH * H].rearrange("p c (h e) -> p c h e", e=VH)
                ac.copy(dst[:, :, :, 0:DK], ms[0:CK, :].rearrange("p (c h e) -> p c h e", c=4, e=DK)) \
                    .then_inc(v_done, 1)

            def take_row(b, n):
                wait(ac, row_ps, b.count(2, n + 1))
                c = slice(0, 512) if n == 0 else slice(512, HQ)
                ac.copy(q_stack[b.parity][3 * GR:STK, c], ms[0:1, 0:c.stop - c.start]).then_inc(row_done, 1)

            def exponentials(b, s, masked):
                wait(ac, st_ps, b.count(NC, s + 1))
                wait(ac, pv_done, b.count(NC, s - 2))
                ac.activation(split(p_sb[s % 3][:, :]), st[s % 2][0:CK, :, 0:HALF], ACT.Exp) \
                    .then_inc(raw_exp if masked else exp_done, 1)

            def masked_exponential(b):
                wait(ac, neg_spread, b.plus(1).count(1))
                t = masked_prob[:, :]
                ac.activation(t, t, ACT.Exp, bias=masked_col[:, :]).then_inc(masked_prob_done, 1)

            ac.wait_ge(sig["const"], 2)
            ac.wait_ge(sig["aggr"], NP)
            rstd_of(mv[:, :, 1], 1.0)
            ac.wait_ge(ld_s, 48)
            ac.activation(a_exp[:, :], small_sb[:, 0, :], ACT.Exp).then_inc(sig["a_exp"], 1)
            ac.wait_ge(ld_w, 16)
            key_high(Batch(None, 0), 0)
            ac.wait_ge(sig["dt_abs"], 1)
            ac.activation(dt_e[:, :, :], dt_d[:, :, :], ACT.Exp, scale=-1.0).then_inc(sig["dt_exp"], 1)
            ac.wait_ge(sig["dt_scaled"], 1)
            ac.activation(d_a[:, :, :], dt_d[:, :, :], ACT.Exp, scale=-1.0).then_inc(sig["da_exp"], 1)
            ac.wait_ge(ld_m, 16)
            for c in range(MH):
                ac.wait_ge(sig["z_ps"], c + 1)
                ac.activation(split(z_s[:, c, :]), st[c][:, :, 0:HALF], ACT.Silu).then_inc(sig["z_done"], 1)
            key_high(Batch(None, 0), 1)
            for n, h in enumerate((1, 0)):
                ac.wait_ge(sig["bc_ps"], n + 1)
                for t, r in ((b_t, slice(0, DS)), (c_t, slice(DS, 2 * DS))):
                    ac.activation(t[:, halves[h]], mx[h][r, 0:HALF], ACT.Silu, bias=conv_b[r]) \
                        .then_inc(sig["bc_done"], 1)
            key_high(Batch(None, 0), 2)
            ac.wait_ge(sig["v_const"], 2)
            for c in range(2):
                take_values(Batch(None, 0), c)
                if c == 1:
                    take_values(Batch(None, 0), 2)
                ac.wait_ge(sig["xc_ps"], c + 1)
                ac.activation(x_s[:, 4 * c:4 * c + 4, :].rearrange("p (a b) d -> p a (b d)", a=2),
                              st[c][0:PT, :, :], ACT.Silu).then_inc(sig["x_done"], 1)
            ac.wait_ge(sig["yg"], 2)
            ac.activation(sq[:, :, :], yg[:, :, :], ACT.Square).then_inc(sig["sq"], 1)
            ac.wait_ge(sig["ss_ps"], 1)
            rstd_of(pv[0:PT, 0:NP], 1.0 / DI)
            key_high(Batch(None, 1), 0)

            ac.wait_ge(sig["aggr"], 2 * NP)
            rstd_of(mv[:, :, 1], 1.0)
            ac.wait_ge(sig["bq"], 1)
            key_high(Batch(None, 1), 1)
            ac.wait_ge(sig["qa_ps"], 1)
            for h in range(2):
                ac.activation(q_all[:, halves[h]], mx[h][:, 0:HALF], ACT.Identity, bias=bq_s[:, NG:NG + 1],
                              scale=SCALE).then_inc(sig["qa"], 1)
            key_high(Batch(None, 1), 2)
            for q in range(NG):
                ac.wait_ge(sig["q_ps"], q + 1)
                wait(ac, sig["q_lo"], q - 1)
                ac.activation(split(q_f[q % 2][:, :]), st[(q + 1) % 2][0:3 * GR, :, 0:HALF], ACT.Identity,
                              bias=bq_s[0:3 * GR, q:q + 1], scale=SCALE).then_inc(sig["q_f"], 1)

            def iteration(i, masked):
                for s in range(NC):
                    if masked and s == 0 and i.within(B):
                        masked_exponential(i)
                    if s == ROW_STEPS[1] and i.plus(1).within(B):
                        take_row(i.plus(1), 1)
                    if i.within(B):
                        exponentials(i, s, masked)
                    if s < NKB and i.plus(2).within(B):
                        key_high(i.plus(2), s)
                    if 5 <= s < 5 + NKB and i.plus(1).within(B):
                        if i.reg is None and i.k == 0 and s == 5:
                            ac.wait_ge(sig["v_const"], 5)
                        take_values(i.plus(1), s - 5)
                    if s == ROW_STEPS[0] and i.plus(1).within(B):
                        take_row(i.plus(1), 0)

            for n in range(2):
                take_row(Batch(None, 0), n)
            by_mask(ac, lambda masked: pipeline(ac, lambda i: iteration(i, masked)))

            ac.wait_ge(sig["aggr"], 3 * NP)
            rstd_of(mv[:, :, 1], 1.0)
            ac.wait_ge(sig["ss_done"], 1)
            rstd_of(ssum[:, :], 1.0 / D)
            ac.wait_ge(ld_f, 16)
            ac.wait_ge(sig["f_ps"], 1)
            ac.activation(split(f_t[:, :]), st[0][:, :, 0:HALF], ACT.Copy, scale=ln1).then_inc(sig["f_t"], 1)
            ac.wait_ge(sig["fq_ps"], 1)
            ac.activation(split(fq_t[:, :]), st[1][:, :, 0:HALF], ACT.Copy, scale=SCALE).then_inc(sig["fq"], 1)
            ac.wait_ge(sig["fv_ps"], 1)
            ac.wait_ge(sig["fv_const"], 3)
            for c in range(2):
                for a in range(2):
                    r = slice(64 * a, 64 * a + S)
                    dst = fv[r, 4 * c:4 * c + 4, a, 0:VH * H].rearrange("p c (h e) -> p c h e", e=VH)
                    ac.copy(dst[:, :, :, 0:DK], mx[c][r, :].rearrange("p (c h e) -> p c h e", c=4, e=DK)) \
                        .then_inc(sig["fv"], 1)
            ac.wait_ge(sig["fk"], 1)
            ac.copy(fk_hi[:, :], fk_t[:, :]).then_inc(sig["fk_hi"], 1)
            for j in range(NP):
                for a, blocks in enumerate((sig["fqb_even"], sig["fqb_odd"])):
                    ac.wait_ge(blocks, j + 1)
                    wait(ac, sig["fmx_ps"], 2 * j + a - 3)
                    ac.copy(fqb_hi[2 * (j % 2) + a][:, :], fqb[2 * j + a][:, :]).then_inc(sig["fq_hi"], 1)

            def self_take_row(j):
                for n in range(2):
                    ac.wait_ge(sig["frow_ps"], 2 * j + n + 1)
                    wait(ac, sig["fst_ps"], j - 1)
                    c = slice(0, 512) if n == 0 else slice(512, HQ)
                    ac.copy(f_row[j % 2][:, c], mx[0][0:2, 0:c.stop - c.start]).then_inc(sig["frow"], 1)

            self_take_row(0)
            for j in range(NP):
                if j + 1 < NP:
                    self_take_row(j + 1)
                ac.wait_ge(sig["fst_ps"], j + 1)
                wait(ac, sig["fpv_ps"], j - 1)
                ac.activation(split(fp[j % 2][:, :]), st[j % 2][:, :, 0:HALF], ACT.Exp).then_inc(sig["fexp"], 1)

            ac.wait_ge(sig["ss_done"], 2)
            rstd_of(ssum[:, :], 1.0 / D)
            ac.wait_ge(sig["r2_ps"], 1)
            ac.activation(split(r2_t[:, :]), st[0][:, :, 0:HALF], ACT.Copy, scale=ln2).then_inc(sig["r2"], 1)
            ac.wait_ge(sig["gap"], 1)
            ac.activation(e2[:, :], gap2[:, :], ACT.Exp).then_inc(sig["gexp"], 1)
            for g in range(4 * NE):
                ac.wait_ge(sig["ab_ps"], g + 1)
                wait(ac, sig["hid"], g - 1)
                ac.activation(silu_a[g % 2][:, :], st[g % 2][:, 0, 0:HALF], ACT.Silu).then_inc(sig["silu"], 1)

        @block.gpsimd
        def _(po):
            def value_ones(t, s, count):
                po.memset(t, 0.0).then_inc(s, 1)
                po.wait_ge(s, count)
                po.memset(t.rearrange("p c (h e) -> p c h e", e=VH)[:, :, :, DK:VH], 1.0).then_inc(s, 1)
                po.wait_ge(s, count + 1)

            value_ones(v_sb[0][:, :, :], sig["v_const"], 1)
            po.wait_ge(ld_m, 16)
            po.wait_ge(ld_s, 48)
            po.tensor_tensor(w_conv[:, :, :], conv_sb[:, :, :],
                             bc(w_in[:, DI:DI + CONV], [128, TAPS, CONV], 1), ALU.mult).then_inc(sig["w_conv"], 1)
            for h in range(MH):
                po.tensor_scalar(w_outn[:, h, :], w_out[:, h * D:(h + 1) * D], col(norm_w, h), None, ALU.mult) \
                    .then_inc(sig["w_outn"], 1)
            po.wait_ge(ld_c, 16)
            for h in range(MH):
                po.wait_ge(sig["w_outn"], MH)
                po.tensor_scalar(d_ident[:, h, :], ident[0:PT, 0:PT], small_sb[:, 2, h:h + 1], None, ALU.mult) \
                    .then_inc(sig["d_ident"], 1)
            po.wait_ge(sig["d_ident"], MH)
            po.memset(k_stack[0][3 * GR:STK, :, :].bitcast(F32), 1.0).then_inc(sig["v_const"], 1)
            po.wait_ge(sig["v_const"], 3)

            def block_queries(b):
                wait(po, mx_ps, b.plus(-1).count(NU))
                po.tensor_tensor(q_blk[b.parity][:, :].rearrange("p (h q) -> p h q", h=H),
                                 bc(q_all[:, bass.ds(b.count(S), S)].bitcast(F32), [D, H, S], 1),
                                 bc(head_mask, [D, H, S], 2), ALU.mult).then_inc(q_blk_done, 1)
                wait(po, q_blk_done, b.plus(1).count(1))

            def stack_queries(b):
                wait(po, st_ps, b.plus(-1).count(NC))
                po.tensor_tensor(q_stack[b.parity][0:3 * GR, :].rearrange("p (g h q) -> p g h q", g=NG, h=GH),
                                 bc(q_parts[:, :, bass.ds(b.count(S), S)].bitcast(F32), [3 * GR, NG, GH, S], 2),
                                 bc(group_mask[0:3 * GR], [3 * GR, NG, GH, S], 1, 3), ALU.mult) \
                    .then_inc(q_stack_done, 1)
                wait(po, q_stack_done, b.plus(1).count(1))

            def fold(b):
                wait(po, masked_done, b.plus(1).count(2))
                wait(po, o_done, b.count(1))
                po.tensor_tensor(u_col[:, 0, :], u_mask[:, 0:S], u_mask[:, S:2 * S], ALU.add).then_inc(half_fold, 1)
                wait(po, half_fold, b.count(2, 1))
                po.tensor_tensor(u_col[0:64, 1, :], u_mask[0:64, 3 * S:4 * S], u_mask[0:64, 4 * S:5 * S],
                                 ALU.add).then_inc(half_fold, 1)
                wait(po, half_fold, b.plus(1).count(2))
                po.tensor_tensor(u_col[:, 0, :], u_col[:, 0, :], u_mask[:, 2 * S:3 * S], ALU.add) \
                    .then_inc(fold_done, 1)

            po.wait_ge(sig["x1"], NP)
            value_ones(v_sb[1][:, :, :], sig["v_const"], 4)
            po.wait_ge(sig["qa"], 2)
            block_queries(Batch(None, 0))
            block_queries(Batch(None, 1))
            po.memset(k_stack[1][3 * GR:STK, :, :].bitcast(F32), 1.0).then_inc(sig["v_const"], 1)
            po.wait_ge(sig["v_const"], 6)
            po.memset(u_col[64:128, 1, :], 1.0).then_inc(sig["v_const"], 1)
            po.wait_ge(sig["v_const"], 7)
            po.wait_ge(sig["q_lo"], NG)
            stack_queries(Batch(None, 0))

            def keep_rows():
                raw_rows = kept_scores[:, :].bitcast(I32)
                for u in range(NU):
                    t, k = divmod(u, NKB)
                    first, c = t * 128 % S, slice(k * KB, (k + 1) * KB)
                    po.dma_start(raw_rows, mask_rows[first:first + 128, c]).then_inc(raw_in, 16)
                    po.wait_ge(raw_in, 16 * (u + 1))
                    po.tensor_scalar(kept_rows[:, t, c], raw_rows, 0, 0, ALU.is_equal, ALU.is_equal).then_inc(kept_done, 1)
                    po.wait_ge(kept_done, u + 1)

            def spread_neg(b):
                rows, used = in_register(po, b.plus(1).count(2)), in_register(po, b.count(NC))
                po.wait_ge(flag_done, 1)
                wait(po, row_done, rows)
                wait(po, exp_done, used)
                po.partition_broadcast(masked_prob[:, :], q_stack[b.parity][3 * GR:STK, :].bitcast(F32)) \
                    .then_inc(neg_spread, 1)
                wait(po, neg_spread, b.plus(1).count(1))

            def iteration(i, masked):
                if i.plus(-1).within(B):
                    fold(i.plus(-1))
                if i.plus(2).within(B):
                    block_queries(i.plus(2))
                if i.plus(1).within(B):
                    stack_queries(i.plus(1))
                    if masked:
                        spread_neg(i.plus(1))

            def cross_attention(masked):
                if masked:
                    keep_rows()
                    spread_neg(Batch(None, 0))
                pipeline(po, lambda i: iteration(i, masked))

            by_mask(po, cross_attention)

            po.wait_ge(sig["x2_ps"], 1)
            po.memset(fv[:, :, :, :], 0.0).then_inc(sig["fv_const"], 1)
            po.wait_ge(sig["fv_const"], 1)
            for a in range(2):
                po.wait_ge(sig["fv_const"], a + 1)
                t = fv[64 * a:64 * a + S, :, a, :].rearrange("p c (h e) -> p c h e", e=VH)
                po.memset(t[:, :, :, DK:VH], 1.0).then_inc(sig["fv_const"], 1)
            po.wait_ge(sig["fv_const"], 3)
            po.memset(fc[64:128, 1, :, :], 1.0).then_inc(sig["fv_const"], 1)
            po.wait_ge(sig["fv_const"], 4)

            def even_queries(j):
                po.tensor_tensor(fqb[2 * j][:, :].rearrange("p (h q) -> p h q", h=H),
                                 bc(fq_t[:, 2 * j * S:(2 * j + 1) * S], [D, H, S], 1),
                                 bc(head_mask, [D, H, S], 2), ALU.mult).then_inc(sig["fqb_even"], 1)

            def self_fold(j):
                po.wait_ge(sig["fu"], 4 * j + 4)
                wait(po, sig["fo"], j)
                po.tensor_tensor(fc[:, 0, :, :], fu[:, :, 0:S], fu[:, :, S:2 * S], ALU.add) \
                    .then_inc(sig["ffold_half"], 1)
                po.wait_ge(sig["ffold_half"], 2 * j + 1)
                po.tensor_tensor(fc[0:64, 1, :, :], fu[0:64, :, 3 * S:4 * S], fu[0:64, :, 4 * S:5 * S], ALU.add) \
                    .then_inc(sig["ffold_half"], 1)
                po.wait_ge(sig["ffold_half"], 2 * j + 2)
                po.tensor_tensor(fc[:, 0, :, :], fc[:, 0, :, :], fu[:, :, 2 * S:3 * S], ALU.add) \
                    .then_inc(sig["ffold"], 1)

            po.wait_ge(sig["fq"], 1)
            for j in range(NP):
                even_queries(j)
            for j in range(NP):
                self_fold(j)


def kernel(**inputs):
    import numpy as np
    import concourse.bacc as bacc
    from concourse.bass_utils import run_bass_kernel_spmd

    a = {k: np.asarray(v) for k, v in inputs.items()}
    f32 = np.float32

    def pack(layout, n, **parts):
        t = np.zeros((128, n), f32)
        for name, (at, k) in layout.items():
            p = parts[name].reshape(parts[name].shape[0], -1)
            t[:p.shape[0], at:at + k] = p
        return t

    def value_rows(w):
        t = np.zeros((2, 128) + w.shape[1:], f32)
        for tile, _, _, heads, oc in VGROUPS:
            for n in range(heads):
                r = 32 * tile + VH * n
                head = 3 * tile + n if oc == 0 else 12 + 2 * tile + n
                t[0 if oc == 0 else 1, r:r + DK] = w[head * DK:(head + 1) * DK]
        return np.ascontiguousarray(np.moveaxis(t, 0, 1))

    row = np.arange(128)
    block = np.zeros((128, PVC), f32)
    for tile, _, _, heads, oc in VGROUPS:
        for r in range(32):
            n = min(r // VH, 2)
            if n < heads:
                block[32 * tile + r, oc + n * S:oc + (n + 1) * S] = 1.0
            else:
                block[32 * tile + r, oc:oc + S] = 1.0
    spread = np.zeros((128, 128), f32)
    for r in range(128):
        n = (r % 32) // VH
        spread[r // 32 * 32 + (VH * n + DK if n < 3 else DK), r] = 1.0
    start = np.eye(PT, dtype=f32)
    start[0, 0] = start[S, S] = 0.0
    half = np.zeros((2, 128), f32)
    half[0, 0:S] = half[1, 64:64 + S] = 1.0
    cst = pack(CST, CST_N, ident=np.eye(128, dtype=f32), spread=spread, block=block,
               heads=(row[:, None] // DK == np.arange(H)).astype(f32),
               groups=(row[:, None] % GR // DK == np.arange(GH)).astype(f32),
               start=start, half=half, expert=np.broadcast_to(np.arange(NE, dtype=f32), (128, NE)))

    m = {k[8:]: v for k, v in a.items() if k.startswith("L0_attn_")}
    c = {k[9:]: v for k, v in a.items() if k.startswith("L0_xattn_")}
    f = {k[7:]: v for k, v in a.items() if k.startswith("L0_ffn_")}

    mw = pack(MW, MW_N, w_in=m["in_proj_w"].T, w_out=m["out_proj_w"].T.reshape(2, 128, D).transpose(1, 0, 2),
              norm=m["norm_w"].reshape(2, 128).T, conv_b=m["conv_b"][DI:].reshape(-1, 1))
    wq_t, bq = c["wq"].T, c["bq"]
    wq3 = np.stack([np.concatenate([wq_t[:, g * GR:(g + 1) * GR]] * 3, axis=1) for g in range(NG)], axis=1)
    bq3 = np.stack([np.concatenate([bq[g * GR:(g + 1) * GR]] * 3) for g in range(NG)], axis=1)
    xw = pack(XW, XW_N, wk=c["wk"].T, wv=c["wv"].T, bk=c["bk"].reshape(-1, 1), wo=value_rows(c["wo"].T),
              bv=value_rows(c["bv"]), wq3=wq3, wq=wq_t, bq3=bq3, bq=bq.reshape(-1, 1))
    fw = pack(FW, FW_N, wq=f["wq"].T, wk=f["wk"].T, wv=f["wv"].T, wo=value_rows(f["wo"].T), gate=f["gate_w"].T,
              ln1=f["ln1_w"].reshape(-1, 1), ln2=f["ln2_w"].reshape(-1, 1),
              w1=f["w1"].transpose(2, 0, 1), w3=f["w3"].transpose(2, 0, 1),
              w2=f["w2"].transpose(2, 0, 1).reshape(NF, 128, NE, D).transpose(1, 2, 0, 3))
    mask = a["mask_1x1xSxS2_if1"].astype(np.int32, copy=False).reshape(S, CTX)
    arrays = {
        "x": a["x"].reshape(TOK, D),
        "ctx_t": np.ascontiguousarray(a["ctx_1024"].reshape(B * CTX, D).T),
        "mask_t": np.ascontiguousarray(mask.reshape(S, NC, CK).transpose(2, 1, 0)),
        "mask_rows": np.tile(mask, (4, 1)),
        "cst": cst, "mw": mw, "xw": xw, "fw": fw,
        "conv_w": np.ascontiguousarray(m["conv_w"][:, 0, :].T),
        "small": np.stack([m["A_log"], m["dt_bias"], m["D_param"]]),
        "rows": np.concatenate([m["conv_b"][:DI], c["bo"]]).reshape(1, DI + D),
    }
    nc = bacc.Bacc("TRN2", target_bir_lowering=False, num_devices=1)
    args = [nc.dram_tensor("in_" + k, v.shape, mybir.dt.from_np(v.dtype), kind="ExternalInput").ap()
            for k, v in arrays.items()]
    y = nc.dram_tensor("out_y", (TOK, D), F32, kind="ExternalOutput").ap()
    build(nc, *args, y)
    r = run_bass_kernel_spmd(nc, [{"in_" + k: v for k, v in arrays.items()}], core_ids=[0])
    return r.results[0]["out_y"].reshape(B, S, D)
```

```python
from contextlib import ExitStack

import concourse.bass as bass
from concourse import mybir

ALU = mybir.AluOpType
ACT = mybir.ActivationFunctionType
AX = mybir.AxisListType.X
F32 = mybir.dt.float32
F32R = mybir.dt.float32r
I32 = mybir.dt.int32
U32 = mybir.dt.uint32
U8 = mybir.dt.uint8

D = 128
B, S = 16, 56
TOK = B * S
PT = 2 * S
NP = B // 2
HALF = TOK // 2
CTX = 1500
CK = 125
NC = CTX // CK
KB = 500
NKB = CTX // KB
H, DK = 16, 8
GH = 4
NG = H // GH
GR = GH * DK
GQ = GH * S
STK = 3 * GR + 1
HQ = H * S
NT = HQ // 128
NU = NT * NKB
VH = DK + 1
VC = VH * (H + 2)
PVC = 5 * S
EPS = 1e-5
MASKED = -1e-9
DI, DS, HD = 256, 64, 128
MH = DI // HD
CONV = DI + 2 * DS
TAPS = 4
NE, FI = 8, 256
NF = FI // 128
SCALE = float(DK) ** -0.5
LN_EXP = "natural_log_exp_and_others"
VGROUPS = [(t, VH * 3 * t, 3 * S * t, 3, 0) for t in range(4)] + \
          [(t, VH * (12 + 2 * t), S * (12 + 2 * t), 2, 3 * S) for t in range(2)]
W_PIECES = NP
W_PIECE = 2 * NE * FI // W_PIECES
MIX_STEPS = {"output": 2, "rms": 3, "input": 4, "logits": 5, "gates": 6}
ROW_STEPS = (9, 11)
VALUE_PARTS = [(slice(0, 128), slice(0, 3 * S)), (slice(0, 64), slice(3 * S, PVC))]


def widths(**kw):
    at, n = {}, 0
    for name, k in kw.items():
        at[name] = (n, k)
        n += k
    return at, n


CST, CST_N = widths(ident=128, spread=128, block=PVC, heads=H, groups=GH, start=PT, half=128, expert=NE)
MW, MW_N = widths(w_in=2 * DI + 2 * DS + MH, w_out=2 * D, norm=2, conv_b=1)
XW, XW_N = widths(wk=D, wv=D, bk=1, wo=2 * D, bv=2, wq3=NG * 3 * GR, wq=D, bq3=NG, bq=1)
FW, FW_N = widths(wq=D, wk=D, wv=D, wo=2 * D, gate=NE, ln1=1, ln2=1, w2=NE * NF * D)


class Batch:

    def __init__(self, reg, k):
        self.reg, self.k, self.parity = reg, k, k % 2

    def plus(self, n):
        return Batch(self.reg, self.k + n)

    def count(self, per, more=0):
        c = self.k * per + more
        return c if self.reg is None else self.reg * (2 * per) + c

    def buffer_count(self, per):
        c = (self.k // 2 + 1) * per
        return c if self.reg is None else self.reg * per + c

    def within(self, last):
        return self.reg is not None or 0 <= self.k < last


def wait(eng, sem, value):
    if not isinstance(value, int) or value > 0:
        eng.wait_ge(sem, value)


def in_register(eng, value):
    return value if isinstance(value, int) else eng.to_reg(value)


def build(nc, x, ctx_t, mask_t, mask_rows, cst_d, mw_d, xw_d, fw_d, w13_d, conv_w, small, rows, out):
    es, context, early, query, cross, late = (ExitStack() for _ in range(6))
    with es:
        def sb(name, shape, dt=F32, where=es):
            return where.enter_context(nc.sbuf_tensor(name, shape, dt))

        def pb(name, shape):
            return es.enter_context(nc.psum_tensor(name, shape, F32))

        def sem(name):
            return es.enter_context(nc.semaphore(name))

        st = [pb(f"st{i}", [128, 2, 512]) for i in range(2)]
        mx = [pb(f"mx{i}", [128, 512]) for i in range(2)]
        pv = pb("pv", [128, 512])
        ms = pb("ms", [128, 512])

        cst = sb("cst", [128, CST_N])
        ident, spread, block_mask, head_mask, group_mask, start_ident, half_rows, expert_id = (
            cst[:, a:a + n] for a, n in CST.values())
        ident_r = sb("ident_r", [128, 128], F32R)
        half_r = sb("half_r", [2, 128], F32R)
        ones = sb("ones", [128, 128])
        eps_col = sb("eps_col", [128, 1])
        xw = sb("xw", [128, XW_N])
        wk_t, wv_t, bk_col, wo_rows, bv_rows, wq3, wq_t, bq3, bq_col = (xw[:, a:a + n] for a, n in XW.values())
        bq_s = sb("bq_s", [128, NG + 1])
        masked_col = sb("masked_col", [128, 1])
        key_masked = sb("key_masked", [CK, NC, S], U8)
        any_masked, flag = sb("any_masked", [CK, 1]), sb("flag", [1, 1], I32)
        row_sb = sb("row_sb", [1, DI + D])
        fw = sb("fw", [128, FW_N])
        fwq, fwk, fwv, fwo, gate_t, ln1, ln2, w2_t = (fw[:, a:a + n] for a, n in FW.values())
        x_sb = sb("x_sb", [PT, NP, D])
        stats, mv = sb("stats", [PT, NP, 6]), sb("mv", [PT, NP, 2])
        lnv, rstd, ssum = sb("lnv", [PT, NP]), sb("rstd", [PT, NP]), sb("ssum", [PT, NP])
        o_all = sb("o_all", [128, 2, TOK])

        ctx_sb = [sb(f"ctx{i}", [D, CTX], where=context) for i in range(2)]
        k_hi = [sb(f"k_hi{i}", [D, CTX], F32R, context) for i in range(2)]
        k_lo = [sb(f"k_lo{i}", [D, CTX], F32R, context) for i in range(2)]
        k_stack = [sb("k_stack0", [STK, NG, CTX], F32R, context), None]
        v_sb = [sb("v0", [CK, NC, VC], where=context), None]

        key_mask = sb("key_mask", [CK, NC, S], I32, early)
        mw = sb("mw", [128, MW_N], where=early)
        w_in, w_out, norm_w, conv_b = (mw[:, a:a + n] for a, n in MW.values())
        conv_sb = sb("conv_sb", [128, TAPS, CONV], where=early)
        w_conv = sb("w_conv", [128, TAPS, CONV], where=early)
        w_outn = sb("w_outn", [128, 2, D], where=early)
        small_sb = sb("small_sb", [PT, 3, MH], where=early)
        a_exp = sb("a_exp", [PT, MH], where=early)
        d_ident = sb("d_ident", [PT, MH, PT], where=early)
        xn = sb("xn", [PT, NP, D], where=early)
        u_tap = [sb(f"u_tap{k}", [D, B, S], where=early) for k in range(TAPS)]
        b_t, c_t = sb("b_t", [DS, TOK], where=early), sb("c_t", [DS, TOK], where=early)
        z_s = sb("z_s", [D, MH, TOK], where=early)
        x_s = sb("x_s", [PT, NP, DI], where=early)
        diag = sb("diag", [PT, NP, MH, PT], where=early)
        decay = sb("decay", [PT, NP * MH, PT], where=early)
        m_t = sb("m_t", [PT, NP, MH, PT], where=early)
        yg = sb("yg", [D, MH, TOK], where=early)
        sq = z_s
        dt_v, dt_e, dt_d, dt_z, dt_w, dt_q, dt_s, d_a = (
            sb(f"dt{i}", [PT, NP, MH], where=early) for i in range(8))
        early.close()

        k_stack[1] = sb("k_stack1", [STK, NG, CTX], F32R, cross)
        v_sb[1] = sb("v1", [CK, NC, VC], where=cross)
        q_stack = [sb(f"q_stack{i}", [STK, HQ], F32R, cross) for i in range(2)]
        q_all = sb("q_all", [D, TOK], F32R, cross)
        q_blk = [sb(f"q_blk{i}", [D, HQ], F32R, cross) for i in range(2)]
        q_parts = sb("q_parts", [3 * GR, NG, TOK], F32R, cross)
        part_max, row_max = sb("part_max", [128, NT, NKB], where=cross), sb("row_max", [128, NT], where=cross)
        neg_max = sb("neg_max", [128, NT], F32R, cross)
        inv = sb("inv", [128, 2, S], where=cross)
        u_mask, u_col = sb("u_mask", [128, PVC], where=cross), sb("u_col", [128, 2, S], where=cross)
        xn2, u2 = sb("xn2", [PT, NP, D], where=query), sb("u2", [D, TOK], where=query)
        q_f = [sb(f"q_f{i}", [3 * GR, TOK], where=query) for i in range(2)]
        query.close()
        p_sb = [sb(f"p{i}", [CK, HQ], where=cross) for i in range(3)]
        kept_rows = sb("kept_rows", [128, NT, CTX], U8, cross)
        kept_scores, masked_prob = sb("kept_scores", [128, KB], where=cross), sb("masked_prob", [128, HQ], where=cross)
        cross.close()
        context.close()

        xn3, sq3, rn3 = (sb(f"ffn{i}", [PT, NP, D], where=late) for i in range(3))
        f_t, fq_t, fk_t, r2_t = (sb(f"ffn_t{i}", [D, TOK], where=late) for i in range(4))
        fk_hi = sb("fk_hi", [D, TOK], F32R, late)
        fv = sb("fv", [128, NP, 2, VC], where=late)
        f_max = sb("f_max", [128, NP, NT, 2], where=late)
        f_neg = sb("f_neg", [128, NP, NT, 2], F32R, late)
        fqb_hi = [sb(f"fqb_hi{i}", [D, HQ], F32R, late) for i in range(4)]
        fqb = [sb(f"fqb{i}", [D, HQ], where=late) for i in range(B)]
        f_row = [sb(f"f_row{i}", [2, HQ], F32R, late) for i in range(2)]
        fp = [sb(f"fp{i}", [128, HQ], where=late) for i in range(2)]
        fu, fc = sb("fu", [128, 2, PVC], where=late), sb("fc", [128, 2, 2, S], where=late)
        f_inv = sb("f_inv", [128, 2, 2, S], where=late)
        h_t = [sb(f"h_t{i}", [128, NF, HALF], where=late) for i in range(2)]
        silu_a = [f_t[:, i * HALF:(i + 1) * HALF] for i in range(2)]
        logits, top = sb("logits", [PT, NP, NE], where=late), sb("top", [PT, NP, 8], where=late)
        top_i, top_f = sb("top_i", [PT, NP, 8], U32, late), sb("top_f", [PT, NP, 2], where=late)
        gap2, e2, den2, r_1, r_2 = (sb(f"gate{i}", [PT, NP], where=late) for i in range(5))
        g_1, g_2, gates = (sb(f"gates{i}", [PT, NP, NE], where=late) for i in range(3))
        acc = sb("acc", [PT, NP, D], where=late)
        w_hi = sb("w_hi", [D, 2 * NE * FI], F32R, late)
        with ExitStack() as loaded:
            w13 = sb("w13", [D, 2 * NE * FI], where=loaded)
        w_lo = sb("w_lo", [D, 2 * NE * FI], F32R, late)
        r2_hi, r2_lo = fqb_hi[:2]
        late.close()

        HP = NP // 2

        def max_bank(b, u):
            if b.reg is None and b.k == 0:
                return (mx[0], mx[1], pv)[u % 3]
            return mx[(NU * b.parity + u) % 2]

        ld_x, ld_c, ld_w, ld_m, ld_s, ld_f, ld_13 = (
            sem(n) for n in ("ld_x", "ld_c", "ld_w", "ld_m", "ld_s", "ld_f", "ld_13"))
        ctx_in = [sem(f"ctx_in{i}") for i in range(2)]
        stacked = [sem(f"stacked{i}") for i in range(2)]
        k_ps, k_hi_done, k_lo_done = sem("k_ps"), sem("k_hi_done"), sem("k_lo_done")
        v_ps, v_done = sem("v_ps"), sem("v_done")
        q_blk_done, q_stack_done = sem("q_blk_done"), sem("q_stack_done")
        mx_ps, mx_read = sem("mx_ps"), sem("mx_read")
        max_done, neg_done = sem("max_done"), sem("neg_done")
        row_ps, row_done = sem("row_ps"), sem("row_done")
        st_ps, exp_done, pv_done = sem("st_ps"), sem("exp_done"), sem("pv_done")
        masked_done, half_fold, fold_done = sem("masked_done"), sem("half_fold"), sem("fold_done")
        den_ps, inv_done, o_done = sem("den_ps"), sem("inv_done"), sem("o_done")
        sig = {n: sem(n) for n in """
            fk_hi fq_hi const v_const stats_done aggr ln_done rstd_done xn u_ps u_mid tap dt_ps dt_in dt_abs dt_exp dt_scaled
            da_exp diag z_ps z_done bc_ps bc_done xc_ps x_done g_ps decay_ps decay m_half m_done y_ps yg sq
            o_ps ss_ps w_conv w_outn a_exp d_ident x1 u2_ps u2 q_ps q_f q_hi q_lo qa_ps qa bq
            x2_ps bias_ps bias x_added squares ss_done rn f_ps f_t fq_ps fq fk_ps fk fv_ps fv fqb_even fqb_odd fmx_ps f_max f_neg frow_ps frow
            fst_ps fexp fpv_ps fu ffold_half ffold fden_ps f_inv fo fo_ps h1 r2_ps r2 r2_hi r2_lo w_hi w_lo lg_ps top gap gexp gates
            ab_ps silu hid w2_ps w2_read fv_const""".split()}
        ld_k, any_done, flag_ps, flag_done = sem("ld_k"), sem("any_done"), sem("flag_ps"), sem("flag_done")
        raw_in, kept_done, part_done = sem("raw_in"), sem("kept_done"), sem("part_done")
        raw_exp, neg_spread, masked_prob_done = sem("raw_exp"), sem("neg_spread"), sem("masked_prob_done")

        def steps(eng, name):
            s, n = sem(name), [0]

            def step(ins):
                ins.then_inc(s, 1)
                n[0] += 1
                eng.wait_ge(s, n[0])
            return step

        def col(t, j):
            return t[:, j:j + 1]

        def bc(ap, shape, *at):
            for i in at:
                ap = ap.unsqueeze(i)
            return ap.broadcast_to(shape)

        flat_tap = [t[:, :, :].rearrange("p b s -> p (b s)") for t in u_tap]
        halves = [slice(0, HALF), slice(HALF, TOK)]

        def split(ap):
            return ap.rearrange("p (h n) -> p h n", h=2)

        half_pairs = [range(0, NP // 2), range(NP // 2, NP)]
        pairs = [slice(0, NP // 2), slice(NP // 2, NP)]
        bank_a = [mx[0][:, :], st[1][:, 0, :]]
        bank_b = [mx[1][:, :], st[1][:, 1, :]]

        block = es.enter_context(nc.Block())

        def pipeline(eng, iteration):
            iteration(Batch(None, 0))
            with eng.Fori(0, 6) as r:
                iteration(Batch(r, 1))
                iteration(Batch(r, 2))
            for k in range(13, B + 1):
                iteration(Batch(None, k))

        def by_mask(eng, cross_attention):
            eng.wait_ge(flag_done, 1)
            with eng.If(eng.value_load(flag[0:1, 0:1]) > 0):
                cross_attention(True)
            with eng.Else():
                cross_attention(False)

        def keys_read(b):
            return b.plus(1).count(NKB) if b.within(B) else B * NKB

        def fo_view(j, a):
            return o_all[:, a, j * PT:(j + 1) * PT]

        def weight_piece(j):
            return slice(j * W_PIECE, (j + 1) * W_PIECE)

        def units_of_step(s):
            return range(3) if s == 0 else range(2 * s + 1, min(2 * s + 3, NU))

        @block.sync
        def _(sp):
            tok = "(j p) d -> p j d"
            sp.dma_start(x_sb[:, :, :], x.rearrange(tok, p=PT)).then_inc(ld_x, 16)
            sp.dma_start(cst[:, :], cst_d).then_inc(ld_c, 16)
            sp.dma_start(key_mask[:, :, :], mask_t).then_inc(ld_k, 16)
            sp.dma_start(mw[:, :], mw_d).then_inc(ld_m, 16)

            def load_ctx(b):
                wait(sp, v_ps, b.plus(-1).count(NKB))
                sp.dma_start(ctx_sb[b.parity][:, :], ctx_t[:, bass.ds(b.count(CTX), CTX)]).then_inc(ctx_in[b.parity], 16)

            def stack_keys(b):
                split_done, used = in_register(sp, b.plus(1).count(NKB)), in_register(sp, b.plus(-1).count(NC))
                wait(sp, k_lo_done, split_done)
                wait(sp, st_ps, used)
                p = b.parity
                for n, part in enumerate((k_hi, k_lo, k_hi)):
                    for q in range(NG):
                        sp.dma_start(k_stack[p][n * GR:(n + 1) * GR, q, :].bitcast(F32),
                                     part[p][q * GR:(q + 1) * GR, :].bitcast(F32)).then_inc(stacked[p], 16)

            sp.dma_start(conv_sb[:, :, :], conv_w.unsqueeze(0).broadcast_to([128, TAPS, CONV])).then_inc(ld_s, 16)
            sp.dma_start(small_sb[:, :, :], small.unsqueeze(0).broadcast_to([PT, 3, MH])).then_inc(ld_s, 16)
            sp.dma_start(row_sb[:, :], rows).then_inc(ld_s, 16)
            sp.dma_start(xw[:, :], xw_d).then_inc(ld_w, 16)
            load_ctx(Batch(None, 0))
            load_ctx(Batch(None, 1))
            sp.dma_start(fw[:, :], fw_d).then_inc(ld_f, 16)
            stack_keys(Batch(None, 0))
            load_ctx(Batch(None, 2))
            wait(sp, sig["x1"], NP)
            stack_keys(Batch(None, 1))

            def iteration(i):
                if i.plus(3).within(B):
                    load_ctx(i.plus(3))
                if i.plus(2).within(B):
                    stack_keys(i.plus(2))

            pipeline(sp, iteration)
            sp.wait_ge(sig["x2_ps"], 2)
            sp.dma_start(w13[:, :], w13_d).then_inc(ld_13, 16)
            wait(sp, sig["w2_read"], NP * NE)
            sp.dma_start(out.rearrange(tok, p=PT), acc[:, :, :]).then_inc(ld_x, 16)
            sp.wait_ge(ld_x, 32)

        @block.tensor
        def _(pe):
            def mm(o, lhs, rhs, start=True, stop=True):
                return pe.matmul(o, lhs, rhs, start=start, stop=stop, skip_group_check=True)

            def key_product(b, n):
                if n == 0:
                    wait(pe, ctx_in[b.parity], b.buffer_count(16))
                    if b.reg is None and b.k == 1:
                        wait(pe, v_done, NKB)
                    elif b.reg is not None or b.k > 1:
                        wait(pe, row_done, b.plus(-1).count(2))
                else:
                    wait(pe, k_lo_done, b.count(NKB, n))
                mm(ms[:, 0:KB], wk_t, ctx_sb[b.parity][:, n * KB:(n + 1) * KB]).then_inc(k_ps, 1)

            def value_product(b, n):
                if n == 0:
                    if b.reg is None and b.k == 0:
                        wait(pe, k_lo_done, NKB)
                    else:
                        wait(pe, k_lo_done, keys_read(b.plus(1)))
                        wait(pe, inv_done, b.plus(-1).count(1))
                else:
                    wait(pe, v_done, b.count(NKB, n))
                for c in range(4):
                    s = (4 * n + c) * CK
                    last = mm(ms[0:CK, c * D:(c + 1) * D], ctx_sb[b.parity][:, s:s + CK], wv_t)
                last.then_inc(v_ps, 1)

            def max_product(b, u):
                t, k = divmod(u, NKB)
                if u == 0:
                    wait(pe, q_blk_done, b.plus(1).count(1))
                    wait(pe, k_hi_done, b.plus(1).count(NKB))
                wait(pe, mx_read, b.count(NU, u - (2 if b.reg is None and b.k == 0 else 1)))
                mm(max_bank(b, u)[:, 0:KB], q_blk[b.parity][:, t * 128:(t + 1) * 128],
                   k_hi[b.parity][:, k * KB:(k + 1) * KB]).then_inc(mx_ps, 1)

            def row_product(b, n):
                wait(pe, neg_done, b.count(2, n + 1))
                if n == 1:
                    wait(pe, row_done, b.count(2, 1))
                elif b.reg is None and b.k == 0:
                    wait(pe, k_lo_done, 2 * NKB)
                else:
                    wait(pe, v_done, b.plus(1).count(NKB))
                ts = range(4) if n == 0 else range(4, NT)
                for t in ts:
                    last = mm(ms[0:1, (t - ts[0]) * 128:(t - ts[0] + 1) * 128], col(neg_max, t), ident_r[:, :])
                last.then_inc(row_ps, 1)

            def score_product(b, s):
                p = b.parity
                if s == 0:
                    wait(pe, stacked[p], b.buffer_count(16 * 3 * NG))
                    wait(pe, q_stack_done, b.plus(1).count(1))
                    wait(pe, row_done, b.plus(1).count(2))
                wait(pe, exp_done, b.count(NC, s - 1))
                for q in range(NG):
                    last = mm(st[s % 2][0:CK, q // 2, (q % 2) * GQ:(q % 2 + 1) * GQ],
                              k_stack[p][:, q, s * CK:(s + 1) * CK], q_stack[p][:, q * GQ:(q + 1) * GQ])
                last.then_inc(st_ps, 1)

            def pv_product(b, s):
                wait(pe, exp_done, b.count(NC, s + 1))
                if s == 0:
                    wait(pe, masked_done, b.count(2))
                    wait(pe, v_done, b.plus(1).count(NKB))
                for t, vc, qc, heads, oc in VGROUPS:
                    last = mm(pv[32 * t:32 * t + 32, oc:oc + heads * S], v_sb[b.parity][:, s, vc:vc + 32],
                              p_sb[s % 3][:, qc:qc + heads * S], start=(s == 0 and oc == 0), stop=(s == NC - 1))
                last.then_inc(pv_done, 1)

            def den_product(b):
                wait(pe, fold_done, b.plus(1).count(1))
                wait(pe, k_lo_done, keys_read(b.plus(3)))
                wait(pe, inv_done, b.count(1))
                mm(ms[:, 0:2 * S], spread, u_col[:, :, :].rearrange("p a q -> p (a q)")).then_inc(den_ps, 1)

            def output_product(c):
                pe.wait_ge(o_done, (c + 1) * B // 2)
                if c == 0:
                    pe.wait_ge(mx_read, B * NU)
                for j in half_pairs[c]:
                    o = bank_a[c][0:PT, (j % HP) * D:(j % HP + 1) * D]
                    mm(o, ones[0:1, 0:PT], row_sb[:, DI:DI + D], stop=False)
                    for a in range(2):
                        last = mm(o, o_all[:, a, j * PT:(j + 1) * PT], wo_rows[:, a * D:(a + 1) * D],
                                  start=False, stop=(a == 1))
                last.then_inc(sig["x2_ps"], 1)

            def normed_transposes(c, bank, out_sig):
                for j in half_pairs[c]:
                    last = pe.transpose(bank[:, (j % HP) * PT:(j % HP + 1) * PT], rn3[:, j, :], ident[0:PT, 0:PT])
                last.then_inc(out_sig, 1)

            def attention_input(c):
                pe.wait_ge(sig["rn"], c + 1)
                normed_transposes(c, bank_b[c], sig["f_ps"])

            def query_key_products(c):
                pe.wait_ge(ld_f, 16)
                pe.wait_ge(sig["f_t"], c + 1)
                mm(bank_b[c][:, 0:HALF], fwq, f_t[:, halves[c]]).then_inc(sig["fq_ps"], 1)
                mm(bank_a[c][:, 0:HALF], fwk, f_t[:, halves[c]]).then_inc(sig["fk_ps"], 1)

            def self_value_products(c):
                pe.wait_ge(sig["fk"], c + 1)
                for j in half_pairs[c]:
                    for a in range(2):
                        s = (2 * j + a) * S
                        last = mm(bank_a[c][64 * a:64 * a + S, (j % HP) * D:(j % HP + 1) * D], f_t[:, s:s + S], fwv)
                last.then_inc(sig["fv_ps"], 1)

            def first_half_stage(s):
                if s == 1:
                    output_product(0)
                if s == 7:
                    attention_input(0)
                if s == 9:
                    query_key_products(0)
                if s == 11:
                    self_value_products(0)

            def iteration(i):
                for s in range(NC):
                    units = units_of_step(s) if i.plus(1).within(B) else ()
                    if s == ROW_STEPS[1] and i.plus(1).within(B):
                        row_product(i.plus(1), 1)
                    if i.within(B):
                        score_product(i, s)
                    for u in units[:2]:
                        max_product(i.plus(1), u)
                    if s < NKB and i.plus(2).within(B):
                        key_product(i.plus(2), s)
                    for u in units[2:]:
                        max_product(i.plus(1), u)
                    if s == 3 and i.plus(-1).within(B):
                        den_product(i.plus(-1))
                    if 5 <= s < 5 + NKB and i.plus(1).within(B):
                        value_product(i.plus(1), s - 5)
                    if s == ROW_STEPS[0] and i.plus(1).within(B):
                        row_product(i.plus(1), 0)
                    if s == 0 and i.plus(-1).within(B):
                        pv_product(i.plus(-1), NC - 1)
                    elif s > 0 and i.within(B):
                        pv_product(i, s - 1)
                    if i.reg is None and i.k == B - 1:
                        first_half_stage(s)

            b0, b1 = Batch(None, 0), Batch(None, 1)
            pe.wait_ge(ld_c, 16)
            pe.wait_ge(sig["xn"], NP)
            for j in range(NP):
                last = pe.transpose(st[0][:, j // 4, (j % 4) * PT:(j % 4 + 1) * PT], xn[:, j, :], ident[0:PT, 0:PT])
            last.then_inc(sig["u_ps"], 1)
            pe.wait_ge(any_done, 1)
            mm(pv[0:1, 0:1], any_masked[:, :], ones[0:CK, 0:1]).then_inc(flag_ps, 1)
            pe.wait_ge(ld_w, 16)
            for a in range(2):
                last = mm(mx[1][0:1, 0:D], col(bv_rows, a), wo_rows[:, a * D:(a + 1) * D], start=(a == 0), stop=(a == 1))
            last.then_inc(sig["bias_ps"], 1)
            key_product(b0, 0)
            pe.wait_ge(sig["u_mid"], 1)
            pe.wait_ge(ld_m, 16)
            for j in range(NP):
                last = mm(mx[0][0:PT, MH * j:MH * (j + 1)], flat_tap[3][:, j * PT:(j + 1) * PT],
                          w_in[:, 2 * DI + 2 * DS:])
            last.then_inc(sig["dt_ps"], 1)
            for c in range(MH):
                for h in range(2):
                    last = mm(st[c][:, h, 0:HALF], w_in[:, c * 128:(c + 1) * 128], flat_tap[3][:, halves[h]])
                last.then_inc(sig["z_ps"], 1)
            key_product(b0, 1)
            pe.wait_ge(sig["w_conv"], 1)
            pe.wait_ge(sig["bias"], 1)
            pe.wait_ge(sig["tap"], TAPS - 1)
            for h in (1, 0):
                if h == 0:
                    pe.wait_ge(sig["dt_in"], 1)
                for k in range(TAPS):
                    last = mm(mx[h][:, 0:HALF], w_conv[:, k, DI:CONV], flat_tap[k][:, halves[h]],
                              start=(k == 0), stop=(k == TAPS - 1))
                last.then_inc(sig["bc_ps"], 1)
            key_product(b0, 2)
            pe.wait_ge(sig["bc_done"], 4)
            for j in range(NP):
                t = slice(j * PT, (j + 1) * PT)
                last = mm(mx[j // 4][0:PT, (j % 4) * PT:(j % 4 + 1) * PT], b_t[:, t], c_t[:, t])
            last.then_inc(sig["g_ps"], 1)
            pe.wait_ge(sig["diag"], 1)
            pe.wait_ge(sig["z_done"], 2)
            for n in range(4):
                mm(st[n // 2][0:PT, n % 2, 0:HALF], ones[0:PT, 0:PT],
                   diag[:, 2 * n:2 * n + 2, :, :].rearrange("p j h t -> p (j h t)")).then_inc(sig["decay_ps"], 1)
            pe.wait_ge(ld_s, 48)
            for j in range(NP):
                if j % 2 == 0:
                    pe.wait_ge(sig["decay"], 4 * (j // 2 + 1))
                o = st[j // 4][0:PT, (j // 2) % 2, (j % 2) * DI:(j % 2 + 1) * DI]
                mm(o, ones[0:1, 0:PT], row_sb[:, 0:DI], stop=False)
                for k in range(TAPS):
                    last = mm(o, flat_tap[k][:, j * PT:(j + 1) * PT], w_conv[:, k, 0:DI],
                              start=False, stop=(k == TAPS - 1))
                if j % 4 == 3:
                    last.then_inc(sig["xc_ps"], 1)
                if j in (1, 3, 5):
                    value_product(b0, j // 2)
            pe.wait_ge(sig["m_done"], 1)
            pe.wait_ge(sig["x_done"], 2)
            for h in range(MH):
                for j in range(NP):
                    last = mm(st[h][:, j // 4, (j % 4) * PT:(j % 4 + 1) * PT], x_s[:, j, h * HD:(h + 1) * HD],
                              m_t[:, j, h, :])
                last.then_inc(sig["y_ps"], 1)
            pe.wait_ge(sig["yg"], 2)
            pe.wait_ge(sig["w_outn"], 2)
            for j in range(NP):
                for h in range(MH):
                    last = mm(mx[j // 4][0:PT, (j % 4) * D:(j % 4 + 1) * D], yg[:, h, j * PT:(j + 1) * PT],
                              w_outn[:, h, :], start=(h == 0), stop=(h == 1))
            last.then_inc(sig["o_ps"], 1)
            pe.wait_ge(sig["sq"], 1)
            for j in range(NP):
                for h in range(MH):
                    last = mm(pv[0:PT, j:j + 1], sq[:, h, j * PT:(j + 1) * PT], ones[:, 0:1],
                              start=(h == 0), stop=(h == 1))
            last.then_inc(sig["ss_ps"], 1)

            key_product(b1, 0)
            pe.wait_ge(sig["xn"], 2 * NP)
            for j in range(NP):
                last = pe.transpose(st[0][:, j // 4, (j % 4) * PT:(j % 4 + 1) * PT], xn2[:, j, :], ident[0:PT, 0:PT])
            last.then_inc(sig["u2_ps"], 1)
            key_product(b1, 1)
            pe.wait_ge(sig["u2"], 1)
            for h in range(2):
                last = mm(mx[h][:, 0:HALF], wq_t, u2[:, halves[h]])
            last.then_inc(sig["qa_ps"], 1)
            key_product(b1, 2)
            for q in range(NG):
                if q >= 2:
                    pe.wait_ge(sig["qa"], 2)
                    for u in (range(3), range(3, 5))[q - 2]:
                        max_product(b0, u)
                wait(pe, sig["q_hi"], q - 1)
                for h in range(2):
                    last = mm(st[(q + 1) % 2][0:3 * GR, h, 0:HALF], wq3[:, q * 3 * GR:(q + 1) * 3 * GR],
                              u2[:, halves[h]])
                last.then_inc(sig["q_ps"], 1)
            for u in range(5, NU):
                max_product(b0, u)
            for n in range(2):
                row_product(b0, n)

            pipeline(pe, iteration)

            def self_max(j):
                if j % HP == 0:
                    pe.wait_ge(sig["fk_hi"], j // HP + 1)
                    pe.wait_ge(sig["fv"], 2 * (j // HP) + 2)
                for a in range(2):
                    pe.wait_ge(sig["fq_hi"], 2 * j + a + 1)
                    wait(pe, sig["f_max"], 2 * j + a - 1)
                    for t in range(NT):
                        last = mm(mx[a][:, t * S:(t + 1) * S], fqb_hi[2 * (j % 2) + a][:, t * 128:(t + 1) * 128],
                                  fk_hi[:, (2 * j + a) * S:(2 * j + a + 1) * S])
                    last.then_inc(sig["fmx_ps"], 1)

            def self_row(j, n):
                if n == 0:
                    pe.wait_ge(sig["f_neg"], j + 1)
                    if j == 0:
                        pe.wait_ge(sig["f_max"], 2 * NP)
                wait(pe, sig["frow"], 2 * j + n)
                ts = range(4) if n == 0 else range(4, NT)
                for t in ts:
                    last = mm(mx[0][0:2, (t - ts[0]) * 128:(t - ts[0] + 1) * 128], f_neg[:, j, t, :], ident_r[:, :])
                last.then_inc(sig["frow_ps"], 1)

            def self_scores(j, h):
                if h == 0:
                    wait(pe, sig["fexp"], j - 1)
                pe.wait_ge(sig["frow"], 2 * j + h + 1)
                o = st[j % 2][:, h, 0:HALF]
                mm(o, half_r[:, :], f_row[j % 2][:, halves[h]], stop=False)
                for a in range(2):
                    last = mm(o[64 * a:64 * a + S], fk_t[:, (2 * j + a) * S:(2 * j + a + 1) * S],
                              fqb[2 * j + a][:, halves[h]], start=False)
                if h == 1:
                    last.then_inc(sig["fst_ps"], 1)

            def self_values(j):
                pe.wait_ge(sig["fexp"], j + 1)
                wait(pe, sig["fu"], 4 * j)
                for a, bank in enumerate((pv, ms)):
                    for t, vc, qc, heads, oc in VGROUPS:
                        last = mm(bank[32 * t:32 * t + 32, oc:oc + heads * S], fv[:, j, a, vc:vc + 32],
                                  fp[j % 2][:, qc:qc + heads * S], start=(oc == 0))
                last.then_inc(sig["fpv_ps"], 1)

            def self_den(j):
                pe.wait_ge(sig["ffold"], j + 1)
                wait(pe, sig["f_inv"], j)
                mm(mx[1][:, 0:4 * S], spread, fc[:, :, :, :].rearrange("p a b q -> p (a b q)")) \
                    .then_inc(sig["fden_ps"], 1)

            self_max(0)
            output_product(1)
            self_max(1)
            attention_input(1)
            self_max(2)
            query_key_products(1)
            self_max(3)
            self_value_products(1)
            for j in range(HP, NP):
                self_max(j)

            def attention_output(c):
                pe.wait_ge(sig["fo"], HP * (c + 1))
                if c == 0:
                    pe.wait_ge(sig["frow"], 2 * NP)
                for j in half_pairs[c]:
                    for a in range(2):
                        last = mm(mx[c][0:PT, (j % HP) * D:(j % HP + 1) * D], fo_view(j, a), fwo[:, a * D:(a + 1) * D],
                                  start=(a == 0), stop=(a == 1))
                last.then_inc(sig["fo_ps"], 1)

            def mixture_input(c):
                pe.wait_ge(sig["rn"], c + 3)
                if c == 1:
                    pe.wait_ge(sig["gates"], 1)
                normed_transposes(c, (st[0][:, 1, :], mx[0][:, :])[c], sig["r2_ps"])

            def gate_logits(c):
                pe.wait_ge(sig["r2"], c + 1)
                for j in half_pairs[c]:
                    last = mm(mx[c][0:PT, (j % HP) * NE:(j % HP + 1) * NE], r2_t[:, j * PT:(j + 1) * PT], gate_t)
                last.then_inc(sig["lg_ps"], 1)

            for n in range(2):
                self_row(0, n)
            for j in range(NP + 2):
                for h in range(2):
                    if j + 1 < NP:
                        self_row(j + 1, h)
                    if j < NP:
                        self_scores(j, h)
                if j == NP - 1:
                    attention_output(0)
                if 1 <= j <= NP:
                    self_values(j - 1)
                if j >= 2:
                    self_den(j - 2)
                if j == NP:
                    mixture_input(0)
            gate_logits(0)

            def expert_in(m, n):
                e, h, g = m % NE, m // NE, NF * m + n
                wait(pe, sig["hid"], g - 1)
                if g == 1:
                    pe.wait_ge(sig["fexp"], NP)
                pe.wait_ge(sig["r2"], h + 1)
                pe.wait_ge(sig["r2_lo"], h + 1)
                pe.wait_ge(sig["w_lo"], W_PIECES)
                for a in range(2):
                    o, at = st[g % 2][:, a, 0:HALF], (a * NE + e) * FI + n * 128
                    mm(o, w_lo[:, at:at + 128], r2_hi[:, halves[h]], stop=False)
                    mm(o, w_hi[:, at:at + 128], r2_lo[:, halves[h]], start=False, stop=False)
                    last = mm(o, w_hi[:, at:at + 128], r2_hi[:, halves[h]], start=False)
                last.then_inc(sig["ab_ps"], 1)

            def expert_out(m):
                e, bank = m % NE, (pv, ms)[m % 2]
                pe.wait_ge(sig["hid"], NF * (m + 1))
                if m < 2:
                    pe.wait_ge(sig["fu"], 4 * NP)
                wait(pe, sig["w2_read"], HP * (m - 1))
                for j in range(HP):
                    for n in range(NF):
                        last = mm(bank[0:PT, j * D:(j + 1) * D], h_t[m % 2][:, n, j * PT:(j + 1) * PT],
                                  w2_t[:, (e * NF + n) * D:(e * NF + n + 1) * D], start=(n == 0), stop=(n == 1))
                last.then_inc(sig["w2_ps"], 1)

            for m in range(2 * NE + 1):
                if m < 2 * NE:
                    for n in range(NF):
                        expert_in(m, n)
                if m > 0:
                    expert_out(m - 1)
                if m == MIX_STEPS["output"]:
                    attention_output(1)
                if m == MIX_STEPS["input"]:
                    mixture_input(1)
                if m == MIX_STEPS["logits"]:
                    gate_logits(1)

        @block.vector
        def _(dv):
            step = steps(dv, "dve_step")
            norms = [0]

            def layer_norm(t, normed, which, meanwhile=None):
                norms[0] += 1
                for j in range(NP):
                    dv.bn_stats(stats[:, j, :], t[:, j, :]).then_inc(sig["stats_done"], 1)
                dv.wait_ge(sig["stats_done"], NP * norms[0])
                for j in range(NP):
                    dv.bn_aggr(mv[:, j, :], stats[:, j, :]).then_inc(sig["aggr"], 1)
                if meanwhile:
                    meanwhile()
                dv.wait_ge(sig["aggr"], NP * norms[0])
                dv.wait_ge(sig["rstd_done"], which)
                for j in range(NP):
                    dv.tensor_scalar(normed[:, j, :], t[:, j, :], mv[:, j, 0:1], rstd[:, j:j + 1], ALU.subtract,
                                     ALU.mult).then_inc(sig["xn"], 1)

            dv.memset(ones[:, :], 1.0).then_inc(sig["const"], 1)
            dv.memset(eps_col[:, :], EPS).then_inc(sig["const"], 1)
            step(dv.memset(masked_col[:, :], MASKED))
            for k in range(TAPS - 1):
                step(dv.memset(u_tap[k][:, :, 0:TAPS - 1 - k], 0.0))

            def key_low(b, n):
                c = slice(n * KB, (n + 1) * KB)
                wait(dv, k_hi_done, b.count(NKB, n + 1))
                dv.scalar_tensor_tensor(out=k_lo[b.parity][:, c], in0=ms[:, 0:KB], scalar=bk_col,
                                        in1=k_hi[b.parity][:, c].bitcast(F32), op0=ALU.add,
                                        op1=ALU.subtract).then_inc(k_lo_done, 1)

            dv.wait_ge(ld_x, 16)
            layer_norm(x_sb, xn, 1)
            dv.wait_ge(ld_k, 16)
            step(dv.tensor_scalar(key_masked[:, :, :], key_mask[:, :, :], 0, None, ALU.is_equal))
            dv.tensor_reduce(any_masked[:, :], key_masked[:, :, :].rearrange("p c q -> p (c q)"), AX, ALU.max) \
                .then_inc(any_done, 1)
            dv.wait_ge(ld_c, 16)
            dv.tensor_copy(ident_r[:, :], ident).then_inc(sig["const"], 1)
            dv.tensor_copy(half_r[:, :], half_rows[0:2]).then_inc(sig["const"], 1)
            dv.wait_ge(ld_w, 16)
            dv.tensor_scalar(bq_s[:, :], xw[:, XW["bq3"][0]:XW["bq3"][0] + NG + 1], SCALE, None,
                             ALU.mult).then_inc(sig["bq"], 1)

            dv.wait_ge(sig["u_ps"], 1)
            dv.tensor_copy(split(flat_tap[3]), st[0][:, :, 0:HALF]).then_inc(sig["u_mid"], 1)
            dv.wait_ge(sig["u_mid"], 1)
            for k in (2, 1, 0):
                d = TAPS - 1 - k
                dv.tensor_copy(u_tap[k][:, :, d:S], u_tap[3][:, :, 0:S - d]).then_inc(sig["tap"], 1)
            key_low(Batch(None, 0), 0)
            dv.wait_ge(flag_ps, 1)
            dv.tensor_copy(flag[:, :], pv[0:1, 0:1]).then_inc(flag_done, 1)
            dv.wait_ge(ld_s, 48)
            dv.wait_ge(sig["bias_ps"], 1)
            dv.tensor_tensor(row_sb[:, DI:DI + D], row_sb[:, DI:DI + D], mx[1][0:1, 0:D], ALU.add) \
                .then_inc(sig["bias"], 1)
            dv.wait_ge(sig["dt_ps"], 1)
            dv.wait_ge(ld_s, 48)
            dv.tensor_tensor(dt_v[:, :, :], mx[0][0:PT, 0:NP * MH].rearrange("p (j h) -> p j h", h=MH),
                             bc(small_sb[:, 1, :], [PT, NP, MH], 1), ALU.add).then_inc(sig["dt_in"], 1)
            dv.wait_ge(sig["dt_in"], 1)
            dv.scalar_tensor_tensor(out=dt_d[:, :, :], in0=dt_v[:, :, :], scalar=-1.0, in1=dt_v[:, :, :],
                                    op0=ALU.mult, op1=ALU.max).then_inc(sig["dt_abs"], 1)
            dv.wait_ge(sig["dt_exp"], 1)
            step(dv.tensor_scalar(dt_z[:, :, :], dt_e[:, :, :], 2.0, None, ALU.add))
            step(dv.reciprocal(dt_z[:, :, :], dt_z[:, :, :]))
            step(dv.tensor_tensor(dt_z[:, :, :], dt_z[:, :, :], dt_e[:, :, :], ALU.mult))
            step(dv.tensor_tensor(dt_w[:, :, :], dt_z[:, :, :], dt_z[:, :, :], ALU.mult))
            step(dv.tensor_scalar(dt_q[:, :, :], dt_w[:, :, :], 1.0 / 17, None, ALU.mult))
            for k in range(15, 2, -2):
                step(dv.scalar_tensor_tensor(out=dt_q[:, :, :], in0=dt_q[:, :, :], scalar=1.0 / k,
                                             in1=dt_w[:, :, :], op0=ALU.add, op1=ALU.mult))
            step(dv.scalar_tensor_tensor(out=dt_q[:, :, :], in0=dt_q[:, :, :], scalar=1.0, in1=dt_z[:, :, :],
                                         op0=ALU.add, op1=ALU.mult))
            step(dv.tensor_scalar(dt_w[:, :, :], dt_v[:, :, :], 0.0, None, ALU.max))
            step(dv.scalar_tensor_tensor(out=dt_s[:, :, :], in0=dt_q[:, :, :], scalar=2.0, in1=dt_w[:, :, :],
                                         op0=ALU.mult, op1=ALU.add))
            dv.wait_ge(sig["a_exp"], 1)
            dv.tensor_tensor(dt_d[:, :, :], dt_s[:, :, :], bc(a_exp[:, :], [PT, NP, MH], 1), ALU.mult) \
                .then_inc(sig["dt_scaled"], 1)
            dv.wait_ge(sig["da_exp"], 1)
            dv.tensor_tensor(diag[:, :, :, :], bc(d_a[:, :, :], [PT, NP, MH, PT], 3),
                             bc(start_ident[0:PT], [PT, NP, MH, PT], 1, 1), ALU.mult).then_inc(sig["diag"], 1)
            key_low(Batch(None, 0), 1)
            key_low(Batch(None, 0), 2)
            for n in range(4):
                dv.wait_ge(sig["decay_ps"], n + 1)
                for k in range(4):
                    dv.tensor_tensor_scan(decay[:, 4 * n + k, :], st[n // 2][0:PT, n % 2, k * PT:(k + 1) * PT],
                                          ident[0:PT, 0:PT], 0.0, ALU.mult, ALU.add).then_inc(sig["decay"], 1)
            dv.wait_ge(sig["g_ps"], 1)
            dv.wait_ge(sig["decay"], NP * MH)
            for j in range(NP):
                for h in range(MH):
                    dv.scalar_tensor_tensor(out=m_t[:, j, h, :], in0=decay[:, MH * j + h, :], scalar=dt_s[:, j, h:h + 1],
                                            in1=mx[j // 4][0:PT, (j % 4) * PT:(j % 4 + 1) * PT], op0=ALU.mult,
                                            op1=ALU.mult).then_inc(sig["m_half"], 1)
            dv.wait_ge(sig["m_half"], NP * MH)
            dv.wait_ge(sig["d_ident"], 2)
            dv.tensor_tensor(m_t[:, :, :, :], m_t[:, :, :, :], bc(d_ident[:, :, :], [PT, NP, MH, PT], 1), ALU.add) \
                .then_inc(sig["m_done"], 1)
            dv.wait_ge(sig["z_done"], 2)
            for h in range(MH):
                dv.wait_ge(sig["y_ps"], h + 1)
                dv.tensor_tensor(split(yg[:, h, :]), st[h][:, :, 0:HALF], split(z_s[:, h, :]), ALU.mult) \
                    .then_inc(sig["yg"], 1)
            dv.wait_ge(sig["o_ps"], 1)
            dv.wait_ge(sig["rstd_done"], 2)
            for j in range(NP):
                dv.scalar_tensor_tensor(out=x_sb[:, j, :], in0=mx[j // 4][0:PT, (j % 4) * D:(j % 4 + 1) * D],
                                        scalar=col(rstd, j), in1=x_sb[:, j, :], op0=ALU.mult,
                                        op1=ALU.add).then_inc(sig["x1"], 1)
            dv.wait_ge(sig["x1"], NP)

            layer_norm(x_sb, xn2, 3, lambda: key_low(Batch(None, 1), 0))
            dv.wait_ge(sig["u2_ps"], 1)
            dv.tensor_copy(split(u2[:, :]), st[0][:, :, 0:HALF]).then_inc(sig["u2"], 1)
            key_low(Batch(None, 1), 1)
            key_low(Batch(None, 1), 2)

            def read_max(b, u, masked):
                t, k = divmod(u, NKB)
                scores = max_bank(b, u)[:, 0:KB]
                part = part_max[:, t, k:k + 1]
                wait(dv, mx_ps, b.count(NU, u + 1))
                if not masked:
                    dv.tensor_reduce(part, scores, AX, ALU.max).then_inc(mx_read, 1)
                    return
                if b.reg is None and b.k == 0:
                    dv.wait_ge(kept_done, NU)
                wait(dv, part_done, b.count(NU, u))
                dv.scalar_tensor_tensor(out=kept_scores[:, :], in0=scores, scalar=-MASKED,
                                        in1=kept_rows[:, t, k * KB:(k + 1) * KB], op0=ALU.add,
                                        op1=ALU.mult).then_inc(mx_read, 1)
                wait(dv, mx_read, b.count(NU, u + 1))
                dv.tensor_reduce(part, kept_scores[:, :], AX, ALU.max).then_inc(part_done, 1)

            def negate_max(b, n, masked):
                t = slice(0, 4) if n == 0 else slice(4, NT)
                wait(dv, part_done if masked else mx_read, b.count(NU, NKB * t.stop))
                dv.tensor_reduce(row_max[:, t], part_max[:, t, :], AX, ALU.max).then_inc(max_done, 1)
                wait(dv, max_done, b.count(2, n + 1))
                dv.tensor_scalar(neg_max[:, t], row_max[:, t], -1.0, -MASKED if masked else None, ALU.mult,
                                 *([ALU.add] if masked else [])).then_inc(neg_done, 1)

            def mask_probs(b, s):
                exps, spreads = in_register(dv, b.count(NC, s + 1)), in_register(dv, b.plus(1).count(1))
                dv.wait_ge(flag_done, 1)
                dv.wait_ge(raw_exp, exps)
                if s == 0:
                    dv.wait_ge(masked_prob_done, spreads)
                dv.copy_predicated(p_sb[s % 3][:, :].rearrange("p (h q) -> p h q", h=H),
                                   bc(key_masked[:, s, :], [CK, H, S], 1),
                                   masked_prob[0:CK, :].rearrange("p (h q) -> p h q", h=H)) \
                    .then_inc(exp_done, 1)

            def mask_values(b):
                wait(dv, pv_done, b.plus(1).count(NC))
                wait(dv, fold_done, b.count(1))
                for r, c in VALUE_PARTS:
                    dv.tensor_tensor(u_mask[r, c], pv[r, c], block_mask[r, c], ALU.mult).then_inc(masked_done, 1)

            def divide(b):
                wait(dv, den_ps, b.plus(1).count(1))
                dv.reciprocal(inv[:, :, :], ms[:, 0:2 * S].rearrange("p (a q) -> p a q", a=2)).then_inc(inv_done, 1)
                wait(dv, inv_done, b.plus(1).count(1))
                dv.tensor_tensor(o_all[:, :, bass.ds(b.count(S), S)], u_col[:, :, :], inv[:, :, :], ALU.mult) \
                    .then_inc(o_done, 1)

            def iteration(i, masked):
                if masked and i.plus(-1).within(B):
                    mask_probs(i.plus(-1), NC - 1)
                for s in range(NC):
                    if i.plus(1).within(B):
                        if s == 6:
                            negate_max(i.plus(1), 0, masked)
                        for u in units_of_step(s):
                            read_max(i.plus(1), u, masked)
                        if s == 10:
                            negate_max(i.plus(1), 1, masked)
                    if s < NKB and i.plus(2).within(B):
                        key_low(i.plus(2), s)
                    if s == 3 and i.reg is None and i.k == B:
                        odd_queries(0)
                    if s == 3 and i.plus(-1).within(B):
                        divide(i.plus(-1))
                    if s == 3 and i.reg is None and i.k == B:
                        self_max(0)
                    if s == 0 and i.plus(-1).within(B):
                        mask_values(i.plus(-1))
                    elif masked and s > 0 and i.within(B):
                        mask_probs(i, s - 1)
                    if i.reg is None and i.k == B - 1:
                        first_half_stage(s)

            def odd_queries(j):
                dv.wait_ge(sig["fq"], j // HP + 1)
                if j > 0:
                    dv.wait_ge(pv_done, B * NC)
                dv.tensor_tensor(fqb[2 * j + 1][:, :].rearrange("p (h q) -> p h q", h=H),
                                 bc(fq_t[:, (2 * j + 1) * S:(2 * j + 2) * S], [D, H, S], 1),
                                 bc(head_mask, [D, H, S], 2), ALU.mult).then_inc(sig["fqb_odd"], 1)

            def self_max(j):
                for a in range(2):
                    dv.wait_ge(sig["fmx_ps"], 2 * j + a + 1)
                    dv.tensor_reduce(f_max[:, j, :, a], mx[a][:, 0:NT * S].rearrange("p (t k) -> p t k", k=S), AX,
                                     ALU.max).then_inc(sig["f_max"], 1)
                dv.wait_ge(sig["f_max"], 2 * j + 2)
                dv.tensor_scalar(f_neg[:, j, :, :], f_max[:, j, :, :], -1.0, None, ALU.mult).then_inc(sig["f_neg"], 1)

            def self_mask(j):
                dv.wait_ge(sig["fpv_ps"], j + 1)
                wait(dv, sig["ffold"], j)
                for a, bank in enumerate((pv, ms)):
                    for r, c in VALUE_PARTS:
                        dv.tensor_tensor(fu[r, a, c], bank[r, c], block_mask[r, c], ALU.mult).then_inc(sig["fu"], 1)

            def self_divide(j):
                dv.wait_ge(sig["fden_ps"], j + 1)
                dv.reciprocal(f_inv[:, :, :, :].rearrange("p a b q -> p (a b q)"), mx[1][:, 0:4 * S]) \
                    .then_inc(sig["f_inv"], 1)
                dv.wait_ge(sig["f_inv"], j + 1)
                dv.tensor_tensor(o_all[:, :, j * PT:(j + 1) * PT], fc[:, :, :, :].rearrange("p a b q -> p a (b q)"),
                                 f_inv[:, :, :, :].rearrange("p a b q -> p a (b q)"), ALU.mult) \
                    .then_inc(sig["fo"], 1)

            def add_output(c):
                p = pairs[c]
                dv.wait_ge(sig["x2_ps"], c + 1)
                dv.tensor_tensor(x_sb[:, p, :], x_sb[:, p, :], bank_a[c][0:PT, :].rearrange("p (j d) -> p j d", d=D),
                                 ALU.add).then_inc(sig["x_added"], 1)
                dv.wait_ge(sig["x_added"], c + 1)
                for j in half_pairs[c]:
                    dv.bn_stats(stats[:, j, :], x_sb[:, j, :]).then_inc(sig["stats_done"], 1)
                dv.wait_ge(sig["stats_done"], 2 * NP + HP * (c + 1))
                for j in half_pairs[c]:
                    dv.bn_aggr(mv[:, j, :], stats[:, j, :]).then_inc(sig["aggr"], 1)

            def sum_squares(c, n):
                p = pairs[c]
                dv.tensor_tensor(sq3[:, p, :], xn3[:, p, :], xn3[:, p, :], ALU.mult).then_inc(sig["squares"], 1)
                dv.wait_ge(sig["squares"], n)
                dv.tensor_reduce(ssum[:, p], sq3[:, p, :], AX, ALU.add).then_inc(sig["ss_done"], 1)

            def normalize(c):
                dv.wait_ge(sig["aggr"], 2 * NP + HP * (c + 1))
                dv.wait_ge(sig["rstd_done"], 4 + 2 * c)
                for j in half_pairs[c]:
                    dv.tensor_scalar(xn3[:, j, :], x_sb[:, j, :], mv[:, j, 0:1], rstd[:, j:j + 1], ALU.subtract,
                                     ALU.mult).then_inc(sig["xn"], 1)
                dv.wait_ge(sig["xn"], 2 * NP + HP * (c + 1))
                sum_squares(c, c + 1)

            def rms_scale(c, which):
                p = pairs[c]
                dv.wait_ge(sig["rstd_done"], which)
                dv.tensor_tensor(rn3[:, p, :], xn3[:, p, :], bc(rstd[:, p], [PT, HP, D], 2), ALU.mult) \
                    .then_inc(sig["rn"], 1)

            def take_keys(c):
                dv.wait_ge(sig["fk_ps"], c + 1)
                dv.tensor_copy(fk_t[:, halves[c]], bank_a[c][:, 0:HALF]).then_inc(sig["fk"], 1)

            def first_half_stage(s):
                if s == 2:
                    add_output(0)
                if s == 4:
                    normalize(0)
                if s == 6:
                    rms_scale(0, 5)
                if s == 10:
                    take_keys(0)

            def cross_attention(masked):
                for u in range(NU):
                    read_max(Batch(None, 0), u, masked)
                for n in range(2):
                    negate_max(Batch(None, 0), n, masked)
                pipeline(dv, lambda i: iteration(i, masked))

            by_mask(dv, cross_attention)

            odd_queries(1)
            odd_queries(2)
            add_output(1)
            normalize(1)
            odd_queries(3)
            rms_scale(1, 7)
            self_max(1)
            self_max(2)
            take_keys(1)
            odd_queries(HP)
            self_max(3)
            for j in range(HP, NP):
                if j + 1 < NP:
                    odd_queries(j + 1)
                self_max(j)

            def add_attention(c):
                p = pairs[c]
                dv.wait_ge(sig["fo_ps"], c + 1)
                step(dv.tensor_tensor(xn3[:, p, :], xn3[:, p, :],
                                      mx[c][0:PT, :].rearrange("p (j d) -> p j d", d=D), ALU.add))
                sum_squares(c, c + 3)

            def mixture_norm(c):
                p = pairs[c]
                rms_scale(c, 8 + c)
                step(dv.tensor_tensor(acc[:, p, :], xn3[:, p, :], x_sb[:, p, :], ALU.add))

            def gate_largest(c):
                p = pairs[c]
                dv.wait_ge(sig["lg_ps"], c + 1)
                step(dv.tensor_copy(logits[:, p, :], mx[c][0:PT, 0:HP * NE].rearrange("p (j e) -> p j e", e=NE)))
                for j in half_pairs[c]:
                    dv.max(top[:, j, :], logits[:, j, :]).then_inc(sig["top"], 1)
                for j in half_pairs[c]:
                    dv.wait_ge(sig["top"], 2 * HP * c + j % HP + 1)
                    dv.max_index(top_i[:, j, :], top[:, j, :], logits[:, j, :]).then_inc(sig["top"], 1)
                dv.wait_ge(sig["top"], 2 * HP * (c + 1))
                dv.tensor_tensor(gap2[:, p], top[:, p, 1], top[:, p, 0], ALU.subtract).then_inc(sig["gap"], 1)
                step(dv.tensor_copy(top_f[:, p, :], top_i[:, p, 0:2]))

            def gate_weights(c):
                p, shape = pairs[c], [PT, HP, NE]
                dv.wait_ge(sig["gexp"], c + 1)
                step(dv.tensor_scalar(den2[:, p], e2[:, p], 1.0, None, ALU.add))
                step(dv.reciprocal(r_1[:, p], den2[:, p]))
                step(dv.tensor_tensor(r_2[:, p], e2[:, p], r_1[:, p], ALU.mult))
                for k, (g, r) in enumerate(((g_1, r_1), (g_2, r_2))):
                    step(dv.tensor_tensor(g[:, p, :], bc(expert_id[0:PT], shape, 1), bc(top_f[:, p, k], shape, 2),
                                          ALU.is_equal))
                    step(dv.tensor_tensor(g[:, p, :], g[:, p, :], bc(r[:, p], shape, 2), ALU.mult))
                dv.tensor_tensor(gates[:, p, :], g_1[:, p, :], g_2[:, p, :], ALU.add).then_inc(sig["gates"], 1)
                dv.wait_ge(sig["gates"], c + 1)

            for j in range(NP + 1):
                if j < NP:
                    self_mask(j)
                if j >= 1:
                    self_divide(j - 1)
                if j == NP - 2:
                    add_attention(0)
                if j == NP - 1:
                    mixture_norm(0)

            def hidden(m, n):
                g = NF * m + n
                dv.wait_ge(sig["silu"], g + 1)
                wait(dv, sig["w2_ps"], m - 1)
                dv.tensor_tensor(h_t[m % 2][:, n, :], silu_a[g % 2], st[g % 2][:, 1, 0:HALF], ALU.mult) \
                    .then_inc(sig["hid"], 1)

            def add_expert(m):
                e, h, bank = m % NE, m // NE, (pv, ms)[m % 2]
                dv.wait_ge(sig["w2_ps"], m + 1)
                for j in range(HP):
                    if e > 0:
                        wait(dv, sig["w2_read"], HP * (m - 1) + j + 1)
                    dv.scalar_tensor_tensor(out=acc[:, HP * h + j, :], in0=bank[0:PT, j * D:(j + 1) * D],
                                            scalar=gates[:, HP * h + j, e:e + 1], in1=acc[:, HP * h + j, :],
                                            op0=ALU.mult, op1=ALU.add).then_inc(sig["w2_read"], 1)

            gate_largest(0)
            for m in range(2 * NE + 1):
                if m < 2 * NE:
                    for n in range(NF):
                        hidden(m, n)
                if m == 0:
                    gate_weights(0)
                if m == MIX_STEPS["gates"]:
                    gate_largest(1)
                if m == MIX_STEPS["gates"] + 1:
                    gate_weights(1)
                if m > 0:
                    add_expert(m - 1)
                if m == MIX_STEPS["output"]:
                    add_attention(1)
                if m == MIX_STEPS["rms"]:
                    mixture_norm(1)

        @block.scalar
        def _(ac):
            def rstd_of(n, src, scale, p=slice(0, NP)):
                ac.activation(lnv[:, p], src, ACT.Ln, bias=eps_col[0:PT], scale=scale).then_inc(sig["ln_done"], 1)
                ac.wait_ge(sig["ln_done"], n)
                ac.activation(rstd[:, p], lnv[:, p], ACT.Exp, scale=-0.5).then_inc(sig["rstd_done"], 1)

            def key_high(b, n):
                wait(ac, k_ps, b.count(NKB, n + 1))
                ac.activation(k_hi[b.parity][:, n * KB:(n + 1) * KB], ms[:, 0:KB], ACT.Identity, bias=bk_col) \
                    .then_inc(k_hi_done, 1)

            def take_values(b, n):
                wait(ac, v_ps, b.count(NKB, n + 1))
                dst = v_sb[b.parity][:, 4 * n:4 * n + 4, 0:VH * H].rearrange("p c (h e) -> p c h e", e=VH)
                ac.copy(dst[:, :, :, 0:DK], ms[0:CK, :].rearrange("p (c h e) -> p c h e", c=4, e=DK)) \
                    .then_inc(v_done, 1)

            def take_row(b, n):
                wait(ac, row_ps, b.count(2, n + 1))
                c = slice(0, 512) if n == 0 else slice(512, HQ)
                ac.copy(q_stack[b.parity][3 * GR:STK, c], ms[0:1, 0:c.stop - c.start]).then_inc(row_done, 1)

            def exponentials(b, s, masked):
                wait(ac, st_ps, b.count(NC, s + 1))
                wait(ac, pv_done, b.count(NC, s - 2))
                ac.activation(split(p_sb[s % 3][:, :]), st[s % 2][0:CK, :, 0:HALF], ACT.Exp) \
                    .then_inc(raw_exp if masked else exp_done, 1)

            def masked_exponential(b):
                wait(ac, neg_spread, b.plus(1).count(1))
                t = masked_prob[:, :]
                ac.activation(t, t, ACT.Exp, bias=masked_col[:, :]).then_inc(masked_prob_done, 1)

            ac.preload_act_table_set(LN_EXP)
            ac.wait_ge(sig["const"], 2)
            ac.wait_ge(sig["aggr"], NP)
            rstd_of(1, mv[:, :, 1], 1.0)
            ac.wait_ge(ld_s, 48)
            ac.activation(a_exp[:, :], small_sb[:, 0, :], ACT.Exp).then_inc(sig["a_exp"], 1)
            ac.wait_ge(ld_w, 16)
            key_high(Batch(None, 0), 0)
            ac.wait_ge(sig["dt_abs"], 1)
            ac.activation(dt_e[:, :, :], dt_d[:, :, :], ACT.Exp, scale=-1.0).then_inc(sig["dt_exp"], 1)
            ac.wait_ge(sig["dt_scaled"], 1)
            ac.activation(d_a[:, :, :], dt_d[:, :, :], ACT.Exp, scale=-1.0).then_inc(sig["da_exp"], 1)
            ac.wait_ge(ld_m, 16)
            for c in range(MH):
                ac.wait_ge(sig["z_ps"], c + 1)
                ac.activation(split(z_s[:, c, :]), st[c][:, :, 0:HALF], ACT.Silu).then_inc(sig["z_done"], 1)
            key_high(Batch(None, 0), 1)
            for n, h in enumerate((1, 0)):
                ac.wait_ge(sig["bc_ps"], n + 1)
                for t, r in ((b_t, slice(0, DS)), (c_t, slice(DS, 2 * DS))):
                    ac.activation(t[:, halves[h]], mx[h][r, 0:HALF], ACT.Silu, bias=conv_b[r]) \
                        .then_inc(sig["bc_done"], 1)
            key_high(Batch(None, 0), 2)
            ac.wait_ge(sig["v_const"], 2)
            for c in range(2):
                take_values(Batch(None, 0), c)
                if c == 1:
                    take_values(Batch(None, 0), 2)
                ac.wait_ge(sig["xc_ps"], c + 1)
                ac.activation(x_s[:, 4 * c:4 * c + 4, :].rearrange("p (a b) d -> p a (b d)", a=2),
                              st[c][0:PT, :, :], ACT.Silu).then_inc(sig["x_done"], 1)
            ac.preload_act_table_set(LN_EXP)
            ac.wait_ge(sig["yg"], 2)
            ac.activation(sq[:, :, :], yg[:, :, :], ACT.Square).then_inc(sig["sq"], 1)
            ac.wait_ge(sig["ss_ps"], 1)
            rstd_of(2, pv[0:PT, 0:NP], 1.0 / DI)
            key_high(Batch(None, 1), 0)

            ac.wait_ge(sig["aggr"], 2 * NP)
            rstd_of(3, mv[:, :, 1], 1.0)
            ac.wait_ge(sig["bq"], 1)
            key_high(Batch(None, 1), 1)
            ac.wait_ge(sig["qa_ps"], 1)
            for h in range(2):
                ac.activation(q_all[:, halves[h]], mx[h][:, 0:HALF], ACT.Identity, bias=bq_s[:, NG:NG + 1],
                              scale=SCALE).then_inc(sig["qa"], 1)
            key_high(Batch(None, 1), 2)
            for q in range(NG):
                ac.wait_ge(sig["q_ps"], q + 1)
                wait(ac, sig["q_lo"], q - 1)
                for t, done in ((q_f[q % 2][:, :], "q_f"), (q_parts[:, q, :], "q_hi")):
                    ac.activation(split(t), st[(q + 1) % 2][0:3 * GR, :, 0:HALF], ACT.Identity,
                                  bias=bq_s[0:3 * GR, q:q + 1], scale=SCALE).then_inc(sig[done], 1)

            def iteration(i, masked):
                for s in range(NC):
                    if masked and s == 0 and i.within(B):
                        masked_exponential(i)
                    if s == ROW_STEPS[1] and i.plus(1).within(B):
                        take_row(i.plus(1), 1)
                    if i.within(B):
                        exponentials(i, s, masked)
                    if s < NKB and i.plus(2).within(B):
                        key_high(i.plus(2), s)
                    if 5 <= s < 5 + NKB and i.plus(1).within(B):
                        if i.reg is None and i.k == 0 and s == 5:
                            ac.wait_ge(sig["v_const"], 5)
                        take_values(i.plus(1), s - 5)
                    if s == ROW_STEPS[0] and i.plus(1).within(B):
                        take_row(i.plus(1), 0)
                    if i.reg is None and i.k == B - 1:
                        first_half_stage(s)

            def layer_rstd(c):
                ac.wait_ge(sig["aggr"], 2 * NP + HP * (c + 1))
                rstd_of(4 + 2 * c, mv[:, pairs[c], 1], 1.0, pairs[c])

            def rms_rstd(c, n):
                ac.wait_ge(sig["ss_done"], {5: 1, 7: 2, 8: 3, 9: 4}[n])
                rstd_of(n, ssum[:, pairs[c]], 1.0 / D, pairs[c])

            def take_input(c):
                ac.wait_ge(ld_f, 16)
                ac.wait_ge(sig["f_ps"], c + 1)
                ac.activation(f_t[:, halves[c]], bank_b[c][:, 0:HALF], ACT.Copy, scale=ln1).then_inc(sig["f_t"], 1)

            def take_queries(c):
                ac.wait_ge(sig["fq_ps"], c + 1)
                ac.activation(fq_t[:, halves[c]], bank_b[c][:, 0:HALF], ACT.Copy, scale=SCALE).then_inc(sig["fq"], 1)

            def round_keys(c):
                ac.wait_ge(sig["fk"], c + 1)
                ac.copy(fk_hi[:, halves[c]], fk_t[:, halves[c]]).then_inc(sig["fk_hi"], 1)

            def take_self_values(c):
                ac.wait_ge(sig["fv_const"], 3)
                ac.wait_ge(sig["fv_ps"], c + 1)
                for a in range(2):
                    r = slice(64 * a, 64 * a + S)
                    dst = fv[r, HP * c:HP * (c + 1), a, 0:VH * H].rearrange("p c (h e) -> p c h e", e=VH)
                    ac.copy(dst[:, :, :, 0:DK], bank_a[c][r, :].rearrange("p (c h e) -> p c h e", c=HP, e=DK)) \
                        .then_inc(sig["fv"], 1)

            def round_queries(j):
                for a, blocks in enumerate((sig["fqb_even"], sig["fqb_odd"])):
                    ac.wait_ge(blocks, j + 1)
                    wait(ac, sig["fmx_ps"], 2 * j + a - 3)
                    ac.copy(fqb_hi[2 * (j % 2) + a][:, :], fqb[2 * j + a][:, :]).then_inc(sig["fq_hi"], 1)

            def first_half_stage(s):
                if s == 3:
                    layer_rstd(0)
                if s == 5:
                    rms_rstd(0, 5)
                if s == 8:
                    take_input(0)
                if s == 10:
                    take_queries(0)
                if s == 11:
                    round_keys(0)
                    take_self_values(0)

            for n in range(2):
                take_row(Batch(None, 0), n)
            by_mask(ac, lambda masked: pipeline(ac, lambda i: iteration(i, masked)))

            round_queries(0)
            round_queries(1)
            layer_rstd(1)
            rms_rstd(1, 7)
            round_queries(2)
            take_input(1)
            round_queries(3)
            take_queries(1)
            round_keys(1)
            take_self_values(1)
            for j in range(HP, NP):
                round_queries(j)

            def self_take_row(j):
                for n in range(2):
                    ac.wait_ge(sig["frow_ps"], 2 * j + n + 1)
                    wait(ac, sig["fst_ps"], j - 1)
                    c = slice(0, 512) if n == 0 else slice(512, HQ)
                    ac.copy(f_row[j % 2][:, c], mx[0][0:2, 0:c.stop - c.start]).then_inc(sig["frow"], 1)

            def round_weights(j):
                ac.wait_ge(ld_13, 16)
                ac.copy(w_hi[:, weight_piece(j)], w13[:, weight_piece(j)]).then_inc(sig["w_hi"], 1)

            self_take_row(0)
            for j in range(NP):
                if j + 1 < NP:
                    self_take_row(j + 1)
                ac.wait_ge(sig["fst_ps"], j + 1)
                wait(ac, sig["fpv_ps"], j - 1)
                ac.activation(split(fp[j % 2][:, :]), st[j % 2][:, :, 0:HALF], ACT.Exp).then_inc(sig["fexp"], 1)
                round_weights(j)
            rms_rstd(0, 8)

            def mixture_take(c):
                ac.wait_ge(sig["r2_ps"], c + 1)
                ac.activation(r2_t[:, halves[c]], (st[0][:, 1, 0:HALF], mx[0][:, 0:HALF])[c], ACT.Copy, scale=ln2) \
                    .then_inc(sig["r2"], 1)
                ac.wait_ge(sig["r2"], c + 1)
                ac.copy(r2_hi[:, halves[c]], r2_t[:, halves[c]]).then_inc(sig["r2_hi"], 1)

            def gate_exp(c):
                ac.wait_ge(sig["gap"], c + 1)
                ac.activation(e2[:, pairs[c]], gap2[:, pairs[c]], ACT.Exp).then_inc(sig["gexp"], 1)

            mixture_take(0)
            gate_exp(0)
            for m in range(2 * NE):
                for n in range(NF):
                    g = NF * m + n
                    ac.wait_ge(sig["ab_ps"], g + 1)
                    wait(ac, sig["hid"], g - 1)
                    ac.activation(silu_a[g % 2], st[g % 2][:, 0, 0:HALF], ACT.Silu).then_inc(sig["silu"], 1)
                if m == MIX_STEPS["gates"]:
                    gate_exp(1)
                if m == MIX_STEPS["output"]:
                    rms_rstd(1, 9)
                if m == MIX_STEPS["input"]:
                    mixture_take(1)

        @block.gpsimd
        def _(po):
            def value_ones(t, s, count):
                po.memset(t, 0.0).then_inc(s, 1)
                po.wait_ge(s, count)
                po.memset(t.rearrange("p c (h e) -> p c h e", e=VH)[:, :, :, DK:VH], 1.0).then_inc(s, 1)
                po.wait_ge(s, count + 1)

            value_ones(v_sb[0][:, :, :], sig["v_const"], 1)
            po.wait_ge(ld_m, 16)
            po.wait_ge(ld_s, 48)
            po.tensor_tensor(w_conv[:, :, :], conv_sb[:, :, :],
                             bc(w_in[:, DI:DI + CONV], [128, TAPS, CONV], 1), ALU.mult).then_inc(sig["w_conv"], 1)
            for h in range(MH):
                po.tensor_scalar(w_outn[:, h, :], w_out[:, h * D:(h + 1) * D], col(norm_w, h), None, ALU.mult) \
                    .then_inc(sig["w_outn"], 1)
            po.wait_ge(ld_c, 16)
            for h in range(MH):
                po.wait_ge(sig["w_outn"], MH)
                po.tensor_scalar(d_ident[:, h, :], ident[0:PT, 0:PT], small_sb[:, 2, h:h + 1], None, ALU.mult) \
                    .then_inc(sig["d_ident"], 1)
            po.wait_ge(sig["d_ident"], MH)
            po.memset(k_stack[0][3 * GR:STK, :, :].bitcast(F32), 1.0).then_inc(sig["v_const"], 1)
            po.wait_ge(sig["v_const"], 3)

            def block_queries(b):
                wait(po, mx_ps, b.plus(-1).count(NU))
                po.tensor_tensor(q_blk[b.parity][:, :].rearrange("p (h q) -> p h q", h=H),
                                 bc(q_all[:, bass.ds(b.count(S), S)].bitcast(F32), [D, H, S], 1),
                                 bc(head_mask, [D, H, S], 2), ALU.mult).then_inc(q_blk_done, 1)
                wait(po, q_blk_done, b.plus(1).count(1))

            def stack_queries(b):
                wait(po, st_ps, b.plus(-1).count(NC))
                po.tensor_tensor(q_stack[b.parity][0:3 * GR, :].rearrange("p (g h q) -> p g h q", g=NG, h=GH),
                                 bc(q_parts[:, :, bass.ds(b.count(S), S)].bitcast(F32), [3 * GR, NG, GH, S], 2),
                                 bc(group_mask[0:3 * GR], [3 * GR, NG, GH, S], 1, 3), ALU.mult) \
                    .then_inc(q_stack_done, 1)
                wait(po, q_stack_done, b.plus(1).count(1))

            def fold(b):
                wait(po, masked_done, b.plus(1).count(2))
                wait(po, o_done, b.count(1))
                po.tensor_tensor(u_col[:, 0, :], u_mask[:, 0:S], u_mask[:, S:2 * S], ALU.add).then_inc(half_fold, 1)
                wait(po, half_fold, b.count(2, 1))
                po.tensor_tensor(u_col[0:64, 1, :], u_mask[0:64, 3 * S:4 * S], u_mask[0:64, 4 * S:5 * S],
                                 ALU.add).then_inc(half_fold, 1)
                wait(po, half_fold, b.plus(1).count(2))
                po.tensor_tensor(u_col[:, 0, :], u_col[:, 0, :], u_mask[:, 2 * S:3 * S], ALU.add) \
                    .then_inc(fold_done, 1)

            po.wait_ge(sig["x1"], NP)
            value_ones(v_sb[1][:, :, :], sig["v_const"], 4)
            po.wait_ge(sig["qa"], 2)
            block_queries(Batch(None, 0))
            block_queries(Batch(None, 1))
            for q in range(NG):
                po.wait_ge(sig["q_hi"], q + 1)
                lo = slice(2 * GR, 3 * GR)
                po.tensor_tensor(q_parts[lo, q, :], q_f[q % 2][lo, :], q_parts[lo, q, :].bitcast(F32),
                                 ALU.subtract).then_inc(sig["q_lo"], 1)
            po.memset(u_col[64:128, 1, :], 1.0).then_inc(sig["v_const"], 1)
            po.wait_ge(sig["v_const"], 6)
            po.wait_ge(sig["q_lo"], NG)
            stack_queries(Batch(None, 0))
            po.memset(k_stack[1][3 * GR:STK, :, :].bitcast(F32), 1.0).then_inc(sig["v_const"], 1)
            po.wait_ge(sig["v_const"], 7)

            def keep_rows():
                raw_rows = kept_scores[:, :].bitcast(I32)
                for u in range(NU):
                    t, k = divmod(u, NKB)
                    first, c = t * 128 % S, slice(k * KB, (k + 1) * KB)
                    po.dma_start(raw_rows, mask_rows[first:first + 128, c]).then_inc(raw_in, 16)
                    po.wait_ge(raw_in, 16 * (u + 1))
                    po.tensor_scalar(kept_rows[:, t, c], raw_rows, 0, 0, ALU.is_equal, ALU.is_equal).then_inc(kept_done, 1)
                    po.wait_ge(kept_done, u + 1)

            def spread_neg(b):
                rows, used = in_register(po, b.plus(1).count(2)), in_register(po, b.count(NC))
                po.wait_ge(flag_done, 1)
                wait(po, row_done, rows)
                wait(po, exp_done, used)
                po.partition_broadcast(masked_prob[:, :], q_stack[b.parity][3 * GR:STK, :].bitcast(F32)) \
                    .then_inc(neg_spread, 1)
                wait(po, neg_spread, b.plus(1).count(1))

            def even_queries(j):
                po.wait_ge(sig["fq"], j // HP + 1)
                if j > 0:
                    po.wait_ge(pv_done, B * NC)
                po.tensor_tensor(fqb[2 * j][:, :].rearrange("p (h q) -> p h q", h=H),
                                 bc(fq_t[:, 2 * j * S:(2 * j + 1) * S], [D, H, S], 1),
                                 bc(head_mask, [D, H, S], 2), ALU.mult).then_inc(sig["fqb_even"], 1)

            def iteration(i, masked):
                if i.reg is None and i.k == B:
                    po.wait_ge(sig["fv_const"], 3)
                    even_queries(0)
                    po.wait_ge(sig["fqb_even"], 1)
                if i.plus(-1).within(B):
                    fold(i.plus(-1))
                if i.reg is None and i.k == B - 1:
                    po.wait_ge(fold_done, B - 1)
                    po.wait_ge(pv_done, (B - 1) * NC)
                    po.wait_ge(st_ps, (B - 1) * NC + 1)
                    po.memset(fv[:, :, :, :], 0.0).then_inc(sig["fv_const"], 1)
                    for a in range(2):
                        po.wait_ge(sig["fv_const"], a + 1)
                        t = fv[64 * a:64 * a + S, :, a, :].rearrange("p c (h e) -> p c h e", e=VH)
                        po.memset(t[:, :, :, DK:VH], 1.0).then_inc(sig["fv_const"], 1)
                if i.plus(2).within(B):
                    block_queries(i.plus(2))
                if i.plus(1).within(B):
                    stack_queries(i.plus(1))
                    if masked:
                        spread_neg(i.plus(1))

            def cross_attention(masked):
                if masked:
                    keep_rows()
                    spread_neg(Batch(None, 0))
                pipeline(po, lambda i: iteration(i, masked))

            by_mask(po, cross_attention)

            def self_fold(j):
                po.wait_ge(sig["fu"], 4 * j + 4)
                wait(po, sig["fo"], j)
                po.tensor_tensor(fc[:, 0, :, :], fu[:, :, 0:S], fu[:, :, S:2 * S], ALU.add) \
                    .then_inc(sig["ffold_half"], 1)
                po.wait_ge(sig["ffold_half"], 2 * j + 1)
                po.tensor_tensor(fc[0:64, 1, :, :], fu[0:64, :, 3 * S:4 * S], fu[0:64, :, 4 * S:5 * S], ALU.add) \
                    .then_inc(sig["ffold_half"], 1)
                po.wait_ge(sig["ffold_half"], 2 * j + 2)
                po.tensor_tensor(fc[:, 0, :, :], fc[:, 0, :, :], fu[:, :, 2 * S:3 * S], ALU.add) \
                    .then_inc(sig["ffold"], 1)

            for j in range(1, NP):
                even_queries(j)
            po.wait_ge(sig["fqb_even"], NP)
            po.wait_ge(sig["x2_ps"], 2)
            po.memset(fc[64:128, 1, :, :], 1.0).then_inc(sig["fv_const"], 1)
            po.wait_ge(sig["fv_const"], 4)

            def weights_low(j):
                po.wait_ge(sig["w_hi"], j + 1)
                po.tensor_tensor(w_lo[:, weight_piece(j)], w13[:, weight_piece(j)],
                                 w_hi[:, weight_piece(j)].bitcast(F32), ALU.subtract).then_inc(sig["w_lo"], 1)

            for j in range(NP):
                if j > 0:
                    weights_low(j - 1)
                self_fold(j)
            weights_low(NP - 1)
            for c in range(2):
                po.wait_ge(sig["r2_hi"], c + 1)
                po.tensor_tensor(r2_lo[:, halves[c]], r2_t[:, halves[c]], r2_hi[:, halves[c]].bitcast(F32),
                                 ALU.subtract).then_inc(sig["r2_lo"], 1)


def kernel(**inputs):
    import numpy as np
    import concourse.bacc as bacc
    from concourse.bass_utils import run_bass_kernel_spmd

    a = {k: np.asarray(v) for k, v in inputs.items()}
    f32 = np.float32

    def pack(layout, n, **parts):
        t = np.zeros((128, n), f32)
        for name, (at, k) in layout.items():
            p = parts[name].reshape(parts[name].shape[0], -1)
            t[:p.shape[0], at:at + k] = p
        return t

    def value_rows(w):
        t = np.zeros((2, 128) + w.shape[1:], f32)
        for tile, _, _, heads, oc in VGROUPS:
            for n in range(heads):
                r = 32 * tile + VH * n
                head = 3 * tile + n if oc == 0 else 12 + 2 * tile + n
                t[0 if oc == 0 else 1, r:r + DK] = w[head * DK:(head + 1) * DK]
        return np.ascontiguousarray(np.moveaxis(t, 0, 1))

    row = np.arange(128)
    block = np.zeros((128, PVC), f32)
    for tile, _, _, heads, oc in VGROUPS:
        for r in range(32):
            n = min(r // VH, 2)
            if n < heads:
                block[32 * tile + r, oc + n * S:oc + (n + 1) * S] = 1.0
            else:
                block[32 * tile + r, oc:oc + S] = 1.0
    spread = np.zeros((128, 128), f32)
    for r in range(128):
        n = (r % 32) // VH
        spread[r // 32 * 32 + (VH * n + DK if n < 3 else DK), r] = 1.0
    start = np.eye(PT, dtype=f32)
    start[0, 0] = start[S, S] = 0.0
    half = np.zeros((2, 128), f32)
    half[0, 0:S] = half[1, 64:64 + S] = 1.0
    cst = pack(CST, CST_N, ident=np.eye(128, dtype=f32), spread=spread, block=block,
               heads=(row[:, None] // DK == np.arange(H)).astype(f32),
               groups=(row[:, None] % GR // DK == np.arange(GH)).astype(f32),
               start=start, half=half, expert=np.broadcast_to(np.arange(NE, dtype=f32), (128, NE)))

    m = {k[8:]: v for k, v in a.items() if k.startswith("L0_attn_")}
    c = {k[9:]: v for k, v in a.items() if k.startswith("L0_xattn_")}
    f = {k[7:]: v for k, v in a.items() if k.startswith("L0_ffn_")}

    mw = pack(MW, MW_N, w_in=m["in_proj_w"].T, w_out=m["out_proj_w"].T.reshape(2, 128, D).transpose(1, 0, 2),
              norm=m["norm_w"].reshape(2, 128).T, conv_b=m["conv_b"][DI:].reshape(-1, 1))
    wq_t, bq = c["wq"].T, c["bq"]
    wq3 = np.stack([np.concatenate([wq_t[:, g * GR:(g + 1) * GR]] * 3, axis=1) for g in range(NG)], axis=1)
    bq3 = np.stack([np.concatenate([bq[g * GR:(g + 1) * GR]] * 3) for g in range(NG)], axis=1)
    xw = pack(XW, XW_N, wk=c["wk"].T, wv=c["wv"].T, bk=c["bk"].reshape(-1, 1), wo=value_rows(c["wo"].T),
              bv=value_rows(c["bv"]), wq3=wq3, wq=wq_t, bq3=bq3, bq=bq.reshape(-1, 1))
    fw = pack(FW, FW_N, wq=f["wq"].T, wk=f["wk"].T, wv=f["wv"].T, wo=value_rows(f["wo"].T), gate=f["gate_w"].T,
              ln1=f["ln1_w"].reshape(-1, 1), ln2=f["ln2_w"].reshape(-1, 1),
              w2=f["w2"].transpose(2, 0, 1).reshape(NF, 128, NE, D).transpose(1, 2, 0, 3))
    mask = a["mask_1x1xSxS2_if1"].astype(np.int32, copy=False).reshape(S, CTX)
    arrays = {
        "x": a["x"].reshape(TOK, D),
        "ctx_t": np.ascontiguousarray(a["ctx_1024"].reshape(B * CTX, D).T),
        "mask_t": np.ascontiguousarray(mask.reshape(S, NC, CK).transpose(2, 1, 0)),
        "mask_rows": np.tile(mask, (4, 1)),
        "cst": cst, "mw": mw, "xw": xw, "fw": fw,
        "w13": np.concatenate([f["w1"].reshape(-1, D), f["w3"].reshape(-1, D)]).T.copy(),
        "conv_w": np.ascontiguousarray(m["conv_w"][:, 0, :].T),
        "small": np.stack([m["A_log"], m["dt_bias"], m["D_param"]]),
        "rows": np.concatenate([m["conv_b"][:DI], c["bo"]]).reshape(1, DI + D),
    }
    nc = bacc.Bacc("TRN2", target_bir_lowering=False, num_devices=1)
    args = [nc.dram_tensor("in_" + k, v.shape, mybir.dt.from_np(v.dtype), kind="ExternalInput").ap()
            for k, v in arrays.items()]
    y = nc.dram_tensor("out_y", (TOK, D), F32, kind="ExternalOutput").ap()
    build(nc, *args, y)
    r = run_bass_kernel_spmd(nc, [{"in_" + k: v for k, v in arrays.items()}], core_ids=[0])
    return r.results[0]["out_y"].reshape(B, S, D)
```
